# Optimizing a Trainium2 kernel written in Bass

```python
import numpy as np
import jax
import jax.numpy as jnp

def _softmax(x, axis=-1):
    return jax.nn.softmax(x, axis=axis)

def _gelu(x):
    return jax.nn.gelu(x, approximate=True)

def _silu(x):
    return jax.nn.silu(x)

def _sigmoid(x):
    return jax.nn.sigmoid(x)

def _layernorm(x, axis=-1, eps=1e-05):
    m = jnp.mean(x, axis=axis, keepdims=True)
    v = jnp.var(x, axis=axis, keepdims=True)
    return (x - m) / jnp.sqrt(v + eps)

def _scatter_add(tgt, idx, src, axis=0):
    return tgt.at[idx].add(src)

def _segment_sum(src, seg, n):
    return jax.ops.segment_sum(src, seg, n)
kernel_name = 'mk_macaron_d1_jaxref_r8_7181f5'

def setup_inputs(seed: int=0):
    np.random.seed(seed)
    _w = jnp.asarray

    def _L0_attn_setup():
        import jax, jax.numpy as jnp
        import numpy as np
        import math
        D_MODEL = 128
        N_HEADS = 16
        D_HEAD = D_MODEL // N_HEADS
        MAX_SEQ_LEN = 256
        BASE = 10000.0

        def _rope_tables(L):
            pos = jnp.arange(L, dtype=jnp.float32)[:, None]
            freqs = jnp.exp(-math.log(BASE) * jnp.arange(0, D_HEAD, 2, dtype=jnp.float32) / D_HEAD)
            angles = pos * freqs
            return (jnp.sin(angles), jnp.cos(angles))

        def _apply_rope(x, sin, cos):
            s = sin[None, :, None, :]
            c = cos[None, :, None, :]
            x_even, x_odd = (x[..., ::2], x[..., 1::2])
            rot_even = x_even * c - x_odd * s
            rot_odd = x_even * s + x_odd * c
            return jnp.stack([rot_even, rot_odd], axis=-1).reshape(x.shape)
        key = jax.random.key(seed)
        k0, k1, k2, k3, k4 = jax.random.split(key, 5)
        B, L = (2, 256)
        scale = 1.0 / math.sqrt(D_MODEL)
        return {'x': jax.random.normal(k0, (B, L, D_MODEL), dtype=jnp.float32), 'W_q': jax.random.normal(k1, (D_MODEL, D_MODEL), dtype=jnp.float32) * scale, 'W_k': jax.random.normal(k2, (D_MODEL, D_MODEL), dtype=jnp.float32) * scale, 'W_v': jax.random.normal(k3, (D_MODEL, D_MODEL), dtype=jnp.float32) * scale, 'W_o': jax.random.normal(k4, (D_MODEL, D_MODEL), dtype=jnp.float32) * scale}
    _L0_attn_in = _L0_attn_setup()

    def _L0_ffn_setup():
        import jax, jax.numpy as jnp
        import numpy as np
        DIM, HEADS, FFN, E = (128, 16, 512, 8)
        B, S = (2, 128)
        EPS = 1e-05

        def _ln(x, g, b):
            mu = jnp.mean(x, axis=-1, keepdims=True)
            var = jnp.mean((x - mu) ** 2, axis=-1, keepdims=True)
            return (x - mu) * jax.lax.rsqrt(var + EPS) * g + b
        key = jax.random.key(seed)
        ks = jax.random.split(key, 20)
        sd = 0.02
        d, f = (DIM, FFN)
        return {'x': jax.random.normal(ks[0], (B, S, d), jnp.float32), 'ln1_g': jnp.ones((d,), jnp.float32), 'ln1_b': jnp.zeros((d,), jnp.float32), 'Wqkv': jax.random.normal(ks[1], (d, 3 * d), jnp.float32) * sd, 'bqkv': jnp.zeros((3 * d,), jnp.float32), 'Wo': jax.random.normal(ks[2], (d, d), jnp.float32) * sd, 'bo': jnp.zeros((d,), jnp.float32), 'ln2_g': jnp.ones((d,), jnp.float32), 'ln2_b': jnp.zeros((d,), jnp.float32), 'gate_w': jax.random.normal(ks[3], (d, E), jnp.float32) * sd, 'W1': jax.random.normal(ks[4], (E, d, f), jnp.float32) * sd, 'b1': jnp.zeros((E, f), jnp.float32), 'W2': jax.random.normal(ks[5], (E, f, d), jnp.float32) * sd, 'b2': jnp.zeros((E, d), jnp.float32), 'rW1': jax.random.normal(ks[6], (d, f), jnp.float32) * sd, 'rb1': jnp.zeros((f,), jnp.float32), 'rW2': jax.random.normal(ks[7], (f, d), jnp.float32) * sd, 'rb2': jnp.zeros((d,), jnp.float32), 'coef_w': jax.random.normal(ks[8], (d, 2), jnp.float32) * sd, 'coef_b': jnp.zeros((2,), jnp.float32)}
    _L0_ffn_in = _L0_ffn_setup()
    _d = {'L0_attn_x': _L0_attn_in['x'], 'L0_attn_W_q': _L0_attn_in['W_q'], 'L0_attn_W_k': _L0_attn_in['W_k'], 'L0_attn_W_v': _L0_attn_in['W_v'], 'L0_attn_W_o': _L0_attn_in['W_o'], 'L0_ffn_ln1_g': _L0_ffn_in['ln1_g'], 'L0_ffn_ln1_b': _L0_ffn_in['ln1_b'], 'L0_ffn_Wqkv': _L0_ffn_in['Wqkv'], 'L0_ffn_bqkv': _L0_ffn_in['bqkv'], 'L0_ffn_Wo': _L0_ffn_in['Wo'], 'L0_ffn_bo': _L0_ffn_in['bo'], 'L0_ffn_ln2_g': _L0_ffn_in['ln2_g'], 'L0_ffn_ln2_b': _L0_ffn_in['ln2_b'], 'L0_ffn_gate_w': _L0_ffn_in['gate_w'], 'L0_ffn_W1': _L0_ffn_in['W1'], 'L0_ffn_b1': _L0_ffn_in['b1'], 'L0_ffn_W2': _L0_ffn_in['W2'], 'L0_ffn_b2': _L0_ffn_in['b2'], 'L0_ffn_rW1': _L0_ffn_in['rW1'], 'L0_ffn_rb1': _L0_ffn_in['rb1'], 'L0_ffn_rW2': _L0_ffn_in['rW2'], 'L0_ffn_rb2': _L0_ffn_in['rb2'], 'L0_ffn_coef_w': _L0_ffn_in['coef_w'], 'L0_ffn_coef_b': _L0_ffn_in['coef_b']}
    _x0 = _d['L0_attn_x']
    _d['L0_attn_x'] = jax.random.normal(jax.random.fold_in(jax.random.key(seed), 1), (8, 512, 128), dtype=_x0.dtype)
    del _x0
    return _d

def reference(L0_attn_x, L0_attn_W_q, L0_attn_W_k, L0_attn_W_v, L0_attn_W_o, L0_ffn_ln1_g, L0_ffn_ln1_b, L0_ffn_Wqkv, L0_ffn_bqkv, L0_ffn_Wo, L0_ffn_bo, L0_ffn_ln2_g, L0_ffn_ln2_b, L0_ffn_gate_w, L0_ffn_W1, L0_ffn_b1, L0_ffn_W2, L0_ffn_b2, L0_ffn_rW1, L0_ffn_rb1, L0_ffn_rW2, L0_ffn_rb2, L0_ffn_coef_w, L0_ffn_coef_b):

    def _L0_attn_ref(x, W_q, W_k, W_v, W_o):
        import jax, jax.numpy as jnp
        import numpy as np
        import math
        D_MODEL = 128
        N_HEADS = 16
        D_HEAD = D_MODEL // N_HEADS
        MAX_SEQ_LEN = 256
        BASE = 10000.0

        def _rope_tables(L):
            pos = jnp.arange(L, dtype=jnp.float32)[:, None]
            freqs = jnp.exp(-math.log(BASE) * jnp.arange(0, D_HEAD, 2, dtype=jnp.float32) / D_HEAD)
            angles = pos * freqs
            return (jnp.sin(angles), jnp.cos(angles))

        def _apply_rope(x, sin, cos):
            s = sin[None, :, None, :]
            c = cos[None, :, None, :]
            x_even, x_odd = (x[..., ::2], x[..., 1::2])
            rot_even = x_even * c - x_odd * s
            rot_odd = x_even * s + x_odd * c
            return jnp.stack([rot_even, rot_odd], axis=-1).reshape(x.shape)
        B, L, _ = x.shape
        sin, cos = _rope_tables(L)
        q = (x @ W_q.T).reshape(B, L, N_HEADS, D_HEAD)
        k = (x @ W_k.T).reshape(B, L, N_HEADS, D_HEAD)
        v = (x @ W_v.T).reshape(B, L, N_HEADS, D_HEAD)
        q = _apply_rope(q, sin, cos)
        k = _apply_rope(k, sin, cos)
        scores = jnp.einsum('blhd,bshd->bhls', q, k) / math.sqrt(D_HEAD)
        weights = jax.nn.softmax(scores, axis=-1)
        out = jnp.einsum('bhls,bshd->blhd', weights, v).reshape(B, L, D_MODEL)
        return out @ W_o.T

    def _L0_ffn_ref(x, ln1_g, ln1_b, Wqkv, bqkv, Wo, bo, ln2_g, ln2_b, gate_w, W1, b1, W2, b2, rW1, rb1, rW2, rb2, coef_w, coef_b):
        import jax, jax.numpy as jnp
        import numpy as np
        DIM, HEADS, FFN, E = (128, 16, 512, 8)
        B, S = (2, 128)
        EPS = 1e-05

        def _ln(x, g, b):
            mu = jnp.mean(x, axis=-1, keepdims=True)
            var = jnp.mean((x - mu) ** 2, axis=-1, keepdims=True)
            return (x - mu) * jax.lax.rsqrt(var + EPS) * g + b
        b, s, d = x.shape
        h, dh = (HEADS, d // HEADS)
        xn = _ln(x, ln1_g, ln1_b)
        qkv = xn @ Wqkv + bqkv
        q, k, v = jnp.split(qkv, 3, axis=-1)
        q = q.reshape(b, s, h, dh)
        k = k.reshape(b, s, h, dh)
        v = v.reshape(b, s, h, dh)
        scores = jnp.einsum('bqhd,bkhd->bhqk', q, k) / jnp.sqrt(jnp.float32(dh))
        attn = jax.nn.softmax(scores, axis=-1)
        ctx = jnp.einsum('bhqk,bkhd->bqhd', attn, v).reshape(b, s, d)
        x = x + ctx @ Wo + bo
        xn2 = _ln(x, ln2_g, ln2_b)
        xt = xn2.reshape(b * s, d)
        probs = jax.nn.softmax(xt @ gate_w, axis=-1)
        gate_val = jnp.max(probs, axis=-1, keepdims=True)
        expert_idx = jnp.argmax(probs, axis=-1)
        oh = jax.nn.one_hot(expert_idx, E, dtype=xt.dtype)
        xe = jnp.einsum('te,td->etd', oh, xt)
        he = jax.nn.gelu(jnp.einsum('etd,edf->etf', xe, W1) + b1[:, None, :], approximate=False)
        ye = jnp.einsum('etf,efd->etd', he, W2) + b2[:, None, :]
        moe_out = jnp.einsum('te,etd->td', oh, ye) * gate_val
        rm = jax.nn.gelu(xt @ rW1 + rb1, approximate=False) @ rW2 + rb2
        coef = jax.nn.softmax(xt @ coef_w + coef_b, axis=-1)
        ff = moe_out * coef[:, 0:1] + rm * coef[:, 1:2]
        return x + ff.reshape(b, s, d)
    x = L0_attn_x
    x = x + 0.5 * _L0_ffn_ref(_layernorm(x, axis=-1), L0_ffn_ln1_g, L0_ffn_ln1_b, L0_ffn_Wqkv, L0_ffn_bqkv, L0_ffn_Wo, L0_ffn_bo, L0_ffn_ln2_g, L0_ffn_ln2_b, L0_ffn_gate_w, L0_ffn_W1, L0_ffn_b1, L0_ffn_W2, L0_ffn_b2, L0_ffn_rW1, L0_ffn_rb1, L0_ffn_rW2, L0_ffn_rb2, L0_ffn_coef_w, L0_ffn_coef_b)
    x = x + _L0_attn_ref(_layernorm(x, axis=-1), L0_attn_W_q, L0_attn_W_k, L0_attn_W_v, L0_attn_W_o)
    x = x + 0.5 * _L0_ffn_ref(_layernorm(x, axis=-1), L0_ffn_ln1_g, L0_ffn_ln1_b, L0_ffn_Wqkv, L0_ffn_bqkv, L0_ffn_Wo, L0_ffn_bo, L0_ffn_ln2_g, L0_ffn_ln2_b, L0_ffn_gate_w, L0_ffn_W1, L0_ffn_b1, L0_ffn_W2, L0_ffn_b2, L0_ffn_rW1, L0_ffn_rb1, L0_ffn_rW2, L0_ffn_rb2, L0_ffn_coef_w, L0_ffn_coef_b)
    return x

_drawn_inputs = setup_inputs


def setup_inputs(seed=0):
    import zlib

    import numpy as np

    out = dict(_drawn_inputs(seed))
    spreads = {'L0_ffn_ln1_g': (1.0, 0.6),
     'L0_ffn_ln1_b': (0.0, 0.8),
     'L0_ffn_bqkv': (0.0, 0.581),
     'L0_ffn_bo': (0.0, 0.1),
     'L0_ffn_ln2_g': (1.0, 0.6),
     'L0_ffn_ln2_b': (0.0, 0.8),
     'L0_ffn_b1': (0.0, 0.8),
     'L0_ffn_b2': (0.0, 0.8),
     'L0_ffn_rb1': (0.0, 0.8),
     'L0_ffn_rb2': (0.0, 0.267),
     'L0_ffn_coef_b': (0.0, 0.8)}
    factors = {'L0_ffn_Wqkv': 8.0,
     'L0_ffn_Wo': 3.657,
     'L0_ffn_gate_w': 8.0,
     'L0_ffn_W1': 8.0,
     'L0_ffn_W2': 8.0,
     'L0_ffn_rW1': 3.542,
     'L0_ffn_rW2': 3.149,
     'L0_ffn_coef_w': 8.0}
    for name, (base, spread) in spreads.items():
        noise = np.random.default_rng([zlib.crc32(name.encode()), seed]).standard_normal(out[name].shape)
        drawn = base * np.exp(spread * noise) if base else spread * noise
        out[name] = jnp.asarray(drawn.astype(out[name].dtype))
    for name, factor in factors.items():
        out[name] = (out[name] * factor).astype(out[name].dtype)
    return out
```

```python
from contextlib import ExitStack

import concourse.bass as bass
from concourse import mybir

F32 = mybir.dt.float32
BF16 = mybir.dt.bfloat16
ALU = mybir.AluOpType
ACT = mybir.ActivationFunctionType
AX = mybir.AxisListType

P = 128
BATCH, SEQ, D = 8, 512, 128
HEADS, DH = 16, 8
TOKENS = BATCH * SEQ
TILES = TOKENS // P
TPB = SEQ // P
EXPERTS, FFN = 8, 512
FC = FFN // P
PARTS = 3
EPS = 1e-5
SCALE = float(DH) ** -0.5

Q_SLOTS = [(0, 3), (0, 2), (0, 1)]
K_SLOTS = [0, 0, 0, 1, 1, 2]
SLOT_ROWS = DH * len(K_SLOTS)
MAX_ROW = 96
VW = DH + 1
HALF = HEADS // 2


def guard_first(r):
    return not (isinstance(r, int) and r <= 1)


def bcast_free(ap, n):
    return ap.unsqueeze(2).to_broadcast([ap.shape[0], ap.shape[1], n])


class Core:

    def __init__(self, nc, ctx, args):
        def sb(name, shape, dt=F32):
            return ctx.enter_context(nc.sbuf_tensor(name, shape, dt))

        self.nc, self.a = nc, args
        self.x_tok = sb("x_tok", [P, TILES, D])
        self.y_tok = sb("y_tok", [P, TILES, D])
        self.x_feat = sb("x_feat", [P, TOKENS])
        self.q_stack = [sb(f"q_stack{i}", [P, HEADS, SEQ], BF16) for i in range(2)]
        self.k_stack = [sb(f"k_stack{i}", [P, HEADS, SEQ], BF16) for i in range(2)]
        self.ident = sb("ident", [P, P])
        self.ones_row = sb("ones_row", [1, P])
        self.w_qkv = sb("w_qkv", [P, 3 * D])
        self.b_qk = sb("b_qk", [P, 2])
        self.b_v = sb("b_v", [1, D])
        self.w_o = sb("w_o", [P, D])
        self.b_o = sb("b_o", [1, D])
        self.ln = sb("ln", [P, 4])
        self.a_w = sb("a_w", [P, 6, D])
        self.gate_w = sb("gate_w", [P, EXPERTS + 2])
        self.gate_b = sb("gate_b", [1, EXPERTS + 2])
        self.b_down = sb("b_down", [EXPERTS + 1, D])
        self.w_token = sb("w_token", [P, TILES, EXPERTS + 1])
        self.rank = sb("rank", [P, EXPERTS])

        def dram(name, shape, dt):
            return nc.dram_tensor(name, shape, dt).ap()

        self.sems = []

        self.q_dram = dram("q_dram", [BATCH, HEADS, PARTS, DH, SEQ], BF16)
        self.k_dram = dram("k_dram", [BATCH, HEADS, PARTS, DH, SEQ], BF16)
        self.v_dram = dram("v_dram", [BATCH, P, TPB * HEADS * VW], F32)
        self.o_dram = dram("o_dram", [P, TPB * SEQ], F32)
        self.d_dram = dram("d_dram", [HEADS, SEQ], F32)


    def sem(self, name):
        self.sems.append(self.nc.alloc_semaphore(name))
        return self.sems[-1]

    def end_layer(self):
        self.nc.clear_and_free_semaphores(self.sems)
        self.nc.all_engine_barrier()
        self.sems = []


def setup(k):
    nc, a = k.nc, k.a
    with ExitStack() as ctx:
        loaded = k.sem("loaded")
        zeroed = k.sem("zeroed")
        filled = k.sem("filled")
        block = ctx.enter_context(nc.Block())
        loads = [
            (k.x_tok[:], a["x"].rearrange("b (t p) d -> p (b t) d", p=P)),
            (k.w_qkv[:], a["w_qkv"]), (k.b_qk[:], a["b_qk"]),
            (k.b_v[:], a["b_v"]), (k.w_o[:], a["w_o"]), (k.b_o[:], a["b_o"]),
            (k.ln[:], a["ln"]),
            (k.a_w[:], a["a_w"].rearrange("w i o -> i w o")),
            (k.gate_w[:, 0:EXPERTS], a["gate_w"]), (k.gate_w[:, EXPERTS:], a["coef_w"]),
            (k.b_down[0:EXPERTS, :], a["b2"]), (k.b_down[EXPERTS:, :], a["rb2"]),
        ]

        @block.sync
        def _(sp):
            for dst, src in loads:
                sp.dma_start(dst, src).then_inc(loaded, 16)
            sp.wait_ge(zeroed, 3)
            sp.dma_start(k.gate_b[:, EXPERTS:], a["coef_b"]).then_inc(loaded, 16)
            sp.wait_ge(loaded, 16 * (len(loads) + 1))

        @block.gpsimd
        def _(pool):
            pool.memset(k.ident[:], 0.0).then_inc(filled, 1)
            pool.wait_ge(filled, 1)
            pool.affine_select(out=k.ident[:], in_=k.ident[:], compare_op=ALU.not_equal, fill=1.0,
                               base=0, pattern=[[-1, P]], channel_multiplier=1).then_inc(filled, 1)
            pool.wait_ge(filled, 2)

        @block.vector
        def _(dve):
            dve.memset(k.ones_row[:], 1.0).then_inc(zeroed, 1)
            for e in range(EXPERTS):
                last = dve.memset(k.rank[:, e:e + 1], float(EXPERTS - e))
            last.then_inc(zeroed, 1)
            dve.memset(k.gate_b[:], 0.0).then_inc(zeroed, 1)
            for t in (*k.q_stack, *k.k_stack):
                dve.memset(t[:], 0.0).then_inc(zeroed, 1)
            dve.wait_ge(zeroed, 7)
            for t in k.k_stack:
                dve.memset(t[MAX_ROW:MAX_ROW + PARTS, :, :], 1.0).then_inc(zeroed, 1)
            dve.wait_ge(zeroed, 9)


def layernorm(k, src, dst, name):
    nc = k.nc
    C = 4
    TC = TILES // C
    with ExitStack() as ctx:
        def sb(n, shape):
            return ctx.enter_context(nc.sbuf_tensor(f"{name}_{n}", shape, F32))

        total, var, sd, r, t = (sb(n, [P, TILES]) for n in ("total", "var", "sd", "r", "t"))
        square = sb("square", [P, 2, TC, D])
        done, centered, squared, summed, rooted = (
            k.sem(f"{name}_{n}")
            for n in ("done", "centered", "squared", "summed", "rooted"))
        block = ctx.enter_context(nc.Block())

        @block.scalar
        def _(act):
            for c in range(C):
                act.wait_ge(centered, c + 1)
                if c >= 2:
                    act.wait_ge(summed, c - 1)
                act.activation(square[:, c % 2], dst[:, c * TC:(c + 1) * TC, :],
                               ACT.Square).then_inc(squared, 1)
            act.wait_ge(summed, C + 1)
            act.activation(sd[:], var[:], ACT.Sqrt).then_inc(rooted, 1)

        @block.vector
        def _(dve):
            n = 0
            for c in range(C):
                dve.tensor_reduce(total[:, c * TC:(c + 1) * TC], src[:, c * TC:(c + 1) * TC, :],
                                  AX.X, ALU.add).then_inc(done, 1)
            n += C
            dve.wait_ge(done, n)
            dve.tensor_scalar(total[:], total[:], -1.0 / D, None, ALU.mult).then_inc(done, 1)
            n += 1
            dve.wait_ge(done, n)
            for c in range(C):
                s = slice(c * TC, (c + 1) * TC)
                dve.tensor_tensor(dst[:, s, :], src[:, s, :], bcast_free(total[:, s], D),
                                  ALU.add).then_inc(centered, 1)
            for c in range(C):
                dve.wait_ge(squared, c + 1)
                dve.tensor_reduce(var[:, c * TC:(c + 1) * TC], square[:, c % 2], AX.X,
                                  ALU.add).then_inc(summed, 1)
            dve.wait_ge(summed, C)
            dve.tensor_scalar(var[:], var[:], 1.0 / D, EPS, ALU.mult, ALU.add).then_inc(summed, 1)
            dve.wait_ge(summed, C + 1)
            dve.wait_ge(rooted, 1)
            dve.reciprocal(r[:], sd[:]).then_inc(done, 1)
            for out, x0, x1 in ((t, r, r), (t, t, var)):
                n += 1
                dve.wait_ge(done, n)
                dve.tensor_tensor(out[:], x0[:], x1[:], ALU.mult).then_inc(done, 1)
            n += 1
            dve.wait_ge(done, n)
            dve.tensor_scalar(t[:], t[:], -0.5, 1.5, ALU.mult, ALU.add).then_inc(done, 1)
            n += 1
            dve.wait_ge(done, n)
            dve.tensor_tensor(r[:], r[:], t[:], ALU.mult).then_inc(done, 1)
            n += 1
            dve.wait_ge(done, n)
            dve.wait_ge(centered, C)
            for c in range(C):
                s = slice(c * TC, (c + 1) * TC)
                dve.tensor_tensor(dst[:, s, :], dst[:, s, :], bcast_free(r[:, s], D),
                                  ALU.mult).then_inc(done, 1)
            dve.wait_ge(done, n + C)


def to_features(k, src, gain, bias, name):
    nc = k.nc
    with ExitStack() as ctx:
        ps = ctx.enter_context(nc.psum_tensor(f"{name}_ps", [P, BATCH, SEQ], F32))
        turned = k.sem(f"{name}_turned")
        moved = k.sem(f"{name}_moved")
        block = ctx.enter_context(nc.Block())

        @block.tensor
        def _(pe):
            for t in range(TILES):
                last = pe.transpose(ps[:, t // TPB, (t % TPB) * P:(t % TPB + 1) * P], src[:, t, :],
                                    k.ident[:])
                if t % TPB == TPB - 1:
                    last.then_inc(turned, 1)

        @block.scalar
        def _(act):
            for b in range(0, BATCH, 2):
                act.wait_ge(turned, b + 1)
                act.activation(k.x_feat[:, b * SEQ:(b + 1) * SEQ], ps[:, b], ACT.Identity,
                               scale=gain, bias=bias).then_inc(moved, 1)

        @block.vector
        def _(dve):
            for b in range(1, BATCH, 2):
                dve.wait_ge(turned, b + 1)
                dve.tensor_scalar(k.x_feat[:, b * SEQ:(b + 1) * SEQ], ps[:, b], gain, bias,
                                  ALU.mult, ALU.add).then_inc(moved, 1)
            dve.wait_ge(moved, BATCH)


def project(k, rope, name):
    nc = k.nc
    RING = 3
    with ExitStack() as ctx:
        def sb(n, shape, dt=F32):
            return ctx.enter_context(nc.sbuf_tensor(f"{name}_{n}", shape, dt))

        def sem(n):
            return k.sem(f"{name}_{n}")

        ps = ctx.enter_context(nc.psum_tensor(f"{name}_ps", [P, RING, 2, SEQ], F32))
        ps_v = ctx.enter_context(nc.psum_tensor(f"{name}_psv", [P, 2, SEQ], F32))
        full = sb("full", [P, 2, SEQ])
        rest = sb("rest", [P, 2, SEQ])
        part = sb("part", [P, 2, PARTS, SEQ], BF16)
        v_out = sb("v_out", [P, 2, TPB, HEADS, VW])
        projected, taken, whole, first, less1, second, third = map(sem, (
            "projected", "taken", "whole", "first", "less1", "second", "third"))
        v_done, v_moved, v_ones = map(sem, ("v_done", "v_moved", "v_ones"))
        stored, v_stored = ([sem(f"{n}{i}") for i in range(2)] for n in ("stored", "v_stored"))
        if rope:
            table = sb("table", [P, 2, SEQ])
            turn = sb("turn", [P, 2, 2, SEQ])
            t_loaded, rotated = map(sem, ("t_loaded", "rotated"))
        block = ctx.enter_context(nc.Block())
        items = [(b, s) for b in range(BATCH) for s in range(2)]

        @block.sync
        def _(sp):
            if rope:
                sp.dma_start(table[:], k.a["rope"].rearrange("s p t -> p s t")).then_inc(t_loaded, 16)
                sp.wait_ge(t_loaded, 16)
            for n, (b, s) in enumerate(items):
                sp.wait_ge(third, n + 1)
                for i in range(PARTS):
                    sp.dma_start((k.q_dram, k.k_dram)[s][b, :, i],
                                 part[:, n % 2, i, :]).then_inc(stored[n % 2], 16)
                if s == 1:
                    sp.wait_ge(v_moved, b + 1)
                    sp.dma_start(k.v_dram[b], v_out[:, b % 2].rearrange("p t h w -> p (t h w)")
                                 ).then_inc(v_stored[b % 2], 16)
            for i in range(2):
                sp.wait_ge(stored[i], 16 * PARTS * BATCH)
                sp.wait_ge(v_stored[i], 16 * BATCH // 2)

        @block.tensor
        def _(pe):
            for n, (b, s) in enumerate(items):
                x = k.x_feat[:, b * SEQ:(b + 1) * SEQ]
                if n >= RING:
                    pe.wait_ge(taken, n - RING + 1)
                if rope:
                    pe.matmul(ps[:, n % RING, 0], k.a_w[:, 2 * s, :], x, start=True, stop=True)
                    pe.matmul(ps[:, n % RING, 1], k.a_w[:, 2 * s + 1, :], x, start=True,
                              stop=True).then_inc(projected, 1)
                else:
                    pe.matmul(ps[:, n % RING, 0], k.w_qkv[:, s * D:(s + 1) * D], x, start=True,
                              stop=True).then_inc(projected, 1)
                if s == 0:
                    if b >= 2:
                        pe.wait_ge(v_moved, b - 1)
                    for t in range(TPB):
                        out = ps_v[:, b % 2, t * P:(t + 1) * P]
                        xt = x[:, t * P:(t + 1) * P]
                        if rope:
                            last = pe.matmul(out, xt, k.a_w[:, 4, :], start=True, stop=True)
                        else:
                            pe.matmul(out, xt, k.w_qkv[:, 2 * D:], start=True, stop=False)
                            last = pe.matmul(out, k.ones_row[:], k.b_v[:], start=False, stop=True)
                    last.then_inc(v_done, 1)

        @block.scalar
        def _(act):
            def v_move(b):
                act.wait_ge(v_done, b + 1)
                act.wait_ge(v_ones, 1)
                if b >= 2:
                    act.wait_ge(v_stored[b % 2], 16 * (b // 2))
                act.copy(v_out[:, b % 2, :, :, 0:DH],
                         ps_v[:, b % 2].rearrange("p (t h d) -> p t h d", t=TPB, d=DH)
                         ).then_inc(v_moved, 1)

            def make_whole(n):
                act.wait_ge(projected, n + 1)
                if n >= 2:
                    act.wait_ge(less1, n - 1)
                act.activation(full[:, n % 2], ps[:, n % RING, 0], ACT.Identity,
                               bias=k.b_qk[:, n % 2:n % 2 + 1]).then_inc(taken, 1)

            for n, (b, s) in enumerate(items):
                if not rope:
                    make_whole(n)
                    act.wait_ge(taken, n + 1)
                else:
                    act.wait_ge(whole, n + 1)
                if n >= 2:
                    act.wait_ge(stored[n % 2], 16 * PARTS * (n // 2))
                act.copy(part[:, n % 2, 0, :], full[:, n % 2]).then_inc(first, 1)
                if s == 0:
                    v_move(b)
                act.wait_ge(less1, n + 1)
                act.copy(part[:, n % 2, 1, :], rest[:, n % 2]).then_inc(second, 1)

        @block.vector
        def _(dve):
            dve.memset(v_out[:, :, :, :, DH:], 1.0).then_inc(v_ones, 1)
            if rope:
                dve.wait_ge(t_loaded, 16)

            for n in range(len(items)):
                if rope:
                    dve.wait_ge(projected, n + 1)
                    if n >= 2:
                        dve.wait_ge(whole, n - 1)
                    dve.tensor_tensor(turn[:, n % 2, 0], ps[:, n % RING, 0], table[:, 0],
                                      ALU.mult).then_inc(rotated, 1)
                    dve.tensor_tensor(turn[:, n % 2, 1], ps[:, n % RING, 1], table[:, 1],
                                      ALU.mult).then_inc(taken, 1)
                dve.wait_ge(first, n + 1)
                if n >= 2:
                    dve.wait_ge(third, n - 1)
                dve.tensor_tensor(rest[:, n % 2], full[:, n % 2], part[:, n % 2, 0, :],
                                  ALU.subtract).then_inc(less1, 1)

        @block.gpsimd
        def _(pool):
            for n in range(len(items)):
                if rope:
                    pool.wait_ge(rotated, n + 1)
                    pool.wait_ge(taken, n + 1)
                    if n >= 2:
                        pool.wait_ge(less1, n - 1)
                    pool.tensor_tensor(full[:, n % 2], turn[:, n % 2, 0], turn[:, n % 2, 1],
                                       ALU.add).then_inc(whole, 1)
                pool.wait_ge(second, n + 1)
                pool.tensor_tensor(part[:, n % 2, 2, :], rest[:, n % 2], part[:, n % 2, 1, :],
                                   ALU.subtract).then_inc(third, 1)


def attend(k, name):
    nc = k.nc
    UNITS = 2 * HEADS
    GROUPS = HEADS // 4
    MAXES = HEADS * TPB
    HM = MAXES // 2
    RING = 3
    TURN = (HM + TPB, MAXES + 1)
    LOADS = len(Q_SLOTS) + len(K_SLOTS)
    with ExitStack() as ctx:
        def sb(n, shape, dt=F32):
            return ctx.enter_context(nc.sbuf_tensor(f"{name}_{n}", shape, dt))

        def pb(n, shape):
            return ctx.enter_context(nc.psum_tensor(f"{name}_{n}", shape, F32))

        def sem(n):
            return k.sem(f"{name}_{n}")

        ps_q = pb("ps_q", [P, RING, SEQ])
        ps_k = pb("ps_k", [P, 2, 2, SEQ])
        ps_o = pb("ps_o", [P, SEQ])
        probs = sb("probs", [P, 8, 2, SEQ])
        v_sb = [sb(f"v{i}", [P, TPB, HEADS, VW]) for i in range(2)]
        o_sb = sb("o_sb", [P, GROUPS, SEQ])
        o_num = sb("o_num", [P, SEQ])
        o_den = sb("o_den", [P, SEQ])
        den = sb("den", [P, SEQ // DH])
        maxes = sb("maxes", [P, MAXES])
        m_row = sb("m_row", [HM, P])
        m_rest = sb("m_rest", [HM, P])
        m_part = sb("m_part", [HM, 2, PARTS, P], BF16)
        loaded = [sem("loaded0"), sem("loaded1")]
        v_loaded, o_zeroed = map(sem, ("v_loaded", "o_zeroed"))
        q_scored, q_maxed = map(sem, ("q_scored", "q_maxed"))
        m_turned, m_moved, m_first, m_less, m_second, m_split = map(sem, (
            "m_turned", "m_moved", "m_first", "m_less", "m_second", "m_split"))
        m_loaded = [sem("m_loaded0"), sem("m_loaded1")]
        k_scored, exp_done, pv_done, o_moved = map(sem, ("k_scored", "exp_done", "pv_done", "o_moved"))
        o_stored, n_loaded, d_loaded, d_inverted, d_stored, d_spread, o_divided = map(sem, (
            "o_stored", "n_loaded", "d_loaded", "d_inverted", "d_stored", "d_spread", "o_divided"))
        block = ctx.enter_context(nc.Block())

        def rounds(eng, one):
            one(0, 0, True, False)
            one(1, 1, True, True)
            with eng.Fori(1, BATCH // 2 - 1) as i:
                one(2 * i, 0, True, True)
                one(2 * i + 1, 1, True, True)
            one(BATCH - 2, 0, True, True)
            one(BATCH - 1, 1, True, True)
            one(BATCH, 0, False, True)

        def load_stack(sp, b, par, half):
            h = slice(half * HALF, (half + 1) * HALF)
            row = 0
            for p0, np_ in Q_SLOTS:
                sp.dma_start(k.q_stack[par][row:row + np_ * DH, h, :],
                             k.q_dram[b, h, p0:p0 + np_].rearrange("h i d t -> (i d) h t")
                             ).then_inc(loaded[half], 16)
                row += np_ * DH
            for s, p0 in enumerate(K_SLOTS):
                sp.dma_start(k.k_stack[par][s * DH:(s + 1) * DH, h, :],
                             k.k_dram[b, h, p0].rearrange("h d t -> d h t")
                             ).then_inc(loaded[half], 16)

        def load_max(sp, b, par, half):
            sp.wait_ge(m_split, 2 * b + half + 1)
            for i in range(PARTS):
                sp.dma_start(k.q_stack[par][MAX_ROW + i:MAX_ROW + i + 1, half * HALF:(half + 1) * HALF, :],
                             m_part[:, half, i, :]).then_inc(m_loaded[half], 16)

        o_rows = k.o_dram.rearrange("(g c) (j t) -> j g c t", g=4, j=GROUPS)

        def regroup(sp, count):
            sp.wait_ge(o_moved, GROUPS * count)
            sp.dma_start(k.o_dram, o_sb[:].rearrange("p j t -> p (j t)")).then_inc(o_stored, 16)
            sp.wait_ge(o_stored, 16 * count)
            for j in range(GROUPS):
                sp.dma_start(den[32 * j:32 * j + 32, :],
                             o_rows[j, :, DH, :].rearrange("g (c t) -> g c t", c=DH)
                             ).then_inc(d_loaded, 16)
                sp.dma_start(o_num[32 * j:32 * j + 32, :], o_rows[j, :, 0:DH, :]).then_inc(n_loaded, 16)

        def spread(sp, count):
            sp.wait_ge(d_inverted, count)
            sp.dma_start(k.d_dram.rearrange("h (c t) -> (h c) t", c=DH), den[:]).then_inc(d_stored, 16)
            sp.wait_ge(d_stored, 16 * count)
            sp.dma_start(o_den[:], k.d_dram.unsqueeze(1).to_broadcast([HEADS, DH, SEQ])
                         ).then_inc(d_spread, 16)

        @block.sync
        def _(sp):
            load_stack(sp, 0, 0, 0)
            load_stack(sp, 0, 0, 1)

            def one(r, par, pass1, pass2):
                if pass2:
                    load_max(sp, r - 1, 1 - par, 1)
                if pass1:
                    if pass2:
                        sp.wait_ge(v_loaded, 16 * r)
                        sp.wait_ge(pv_done, 8 * r - 8)
                    sp.dma_start(v_sb[par][:].rearrange("p t h w -> p (t h w)"),
                                 k.v_dram[r]).then_inc(v_loaded, 16)
                if guard_first(r):
                    spread(sp, r - 1)
                last = isinstance(r, int) and r >= BATCH - 1
                if not last:
                    if pass2:
                        sp.wait_ge(k_scored, UNITS * r - UNITS + UNITS // 2)
                    else:
                        sp.wait_ge(loaded[0], 16 * LOADS)
                    load_stack(sp, r + 1, 1 - par, 0)
                if pass1:
                    load_max(sp, r, par, 0)
                if not last:
                    if pass2:
                        sp.wait_ge(k_scored, UNITS * r)
                    else:
                        sp.wait_ge(loaded[1], 16 * LOADS)
                    load_stack(sp, r + 1, 1 - par, 1)
                if pass2:
                    regroup(sp, r)

            rounds(sp, one)
            spread(sp, BATCH)

        @block.tensor
        def _(pe):
            def await_slot(r, u, later):
                if u < RING and not later:
                    return
                before = u - RING
                if before % (MAXES + 2) in TURN:
                    pe.wait_ge(m_moved, 2 * r + (1 if before == TURN[0] else 0))
                else:
                    pe.wait_ge(q_maxed, MAXES * r + before + 1 - (before > TURN[0]) + (before < 0))

            def score_queries(r, par, n, later):
                h, t = n // TPB, n % TPB
                u = n + (n >= TURN[0])
                if n == 0:
                    pe.wait_ge(loaded[0], 16 * LOADS * (r + 1))
                if n == HM:
                    pe.wait_ge(loaded[1], 16 * LOADS * (r + 1))
                await_slot(r, u, later)
                pe.matmul(ps_q[:, u % RING], k.q_stack[par][0:MAX_ROW, h, t * P:(t + 1) * P],
                          k.k_stack[par][0:MAX_ROW, h, :], start=True, stop=True).then_inc(q_scored, 1)

            def turn_maxes(r, half, later):
                u = TURN[half]
                await_slot(r, u, later)
                pe.wait_ge(q_maxed, MAXES * r + HM * (half + 1))
                pe.transpose(ps_q[0:HM, u % RING, 0:P], maxes[:, half * HM:(half + 1) * HM],
                             k.ident[:]).then_inc(m_turned, 1)

            def score_keys(r, par, w):
                b2 = r - 1
                j, half, g = w // 8, w % 8 // 4, w % 4
                head = 4 * j + g
                if w == 0:
                    pe.wait_ge(m_loaded[0], 16 * PARTS * r)
                if w == UNITS // 2:
                    pe.wait_ge(m_loaded[1], 16 * PARTS * r)
                if w >= 2 or guard_first(r):
                    pe.wait_ge(exp_done, UNITS * b2 + w - 1)
                for i in range(2):
                    kt = 2 * half + i
                    last = pe.matmul(ps_k[:, w % 2, i], k.k_stack[1 - par][:, head, kt * P:(kt + 1) * P],
                                     k.q_stack[1 - par][:, head, :], start=True, stop=True)
                last.then_inc(k_scored, 1)

            def apply_v(r, par, v, i):
                b2 = r - 1
                j, half = v // 2, v % 2
                if i == 0:
                    pe.wait_ge(exp_done, UNITS * b2 + 4 * v + 4)
                    if v == 0:
                        pe.wait_ge(o_zeroed, 1)
                        pe.wait_ge(v_loaded, 16 * r)
                    if half == 0 and (j > 0 or guard_first(r)):
                        pe.wait_ge(o_moved, GROUPS * b2 + j)
                for g in range(4):
                    last = pe.matmul(
                        ps_o[32 * g:32 * g + VW, :], v_sb[1 - par][:, 2 * half + i, 4 * j + g, :],
                        probs[:, 4 * half + g, i, :], start=(half == 0 and i == 0),
                        stop=(half == 1 and i == 1), tile_position=(0, 32 * g))
                if i == 1:
                    last.then_inc(pv_done, 1)

            def one(r, par, pass1, pass2):
                for h in range(HEADS):
                    for w in (2 * h, 2 * h + 1):
                        if pass2:
                            score_keys(r, par, w)
                        if pass1:
                            score_queries(r, par, 2 * w, pass2)
                            score_queries(r, par, 2 * w + 1, pass2)
                        if pass2 and w >= 4:
                            if w % 2 == 0:
                                apply_v(r, par, w // 4 - 1, w % 4 // 2)
                    if pass1 and h == HALF:
                        turn_maxes(r, 0, pass2)
                if pass2:
                    apply_v(r, par, 7, 0)
                    apply_v(r, par, 7, 1)
                if pass1:
                    turn_maxes(r, 1, pass2)

            rounds(pe, one)

        @block.vector
        def _(dve):
            dve.memset(ps_o[:], 0.0).then_inc(o_zeroed, 1)

            def invert(count):
                dve.wait_ge(d_loaded, 16 * GROUPS * count)
                dve.reciprocal(den[:], den[:]).then_inc(d_inverted, 1)

            def one(r, par, pass1, pass2):
                for n in range(MAXES):
                    if pass1:
                        dve.wait_ge(q_scored, MAXES * r + n + 1)
                        dve.tensor_reduce(maxes[:, n:n + 1], ps_q[:, (n + (n >= TURN[0])) % RING], AX.X,
                                          ALU.max).then_inc(q_maxed, 1)
                    if guard_first(r) and n == 12:
                        invert(r - 1)

            rounds(dve, one)
            invert(BATCH)

        @block.scalar
        def _(act):
            def move_o(r, j):
                b2 = r - 1
                act.wait_ge(pv_done, 8 * b2 + 2 * j + 2)
                if j == 0 and guard_first(r):
                    act.wait_ge(o_divided, b2)
                act.copy(o_sb[:, j, :], ps_o[:]).then_inc(o_moved, 1)

            def move_max(r, half, later):
                act.wait_ge(m_turned, 2 * r + half + 1)
                if half or later:
                    act.wait_ge(m_split, 2 * r + half)
                act.mul(m_row[:], ps_q[0:HM, TURN[half] % RING, 0:P], -1.0).then_inc(m_first, 1)
                if later:
                    act.wait_ge(m_loaded[half], 16 * PARTS * r)
                act.wait_ge(m_first, 2 * r + half + 1)
                act.mul(m_part[:, half, 0, :], ps_q[0:HM, TURN[half] % RING, 0:P],
                        -1.0).then_inc(m_moved, 1)

            def one(r, par, pass1, pass2):
                for h in range(HEADS):
                    if pass2:
                        b2 = r - 1
                        for w in (2 * h, 2 * h + 1):
                            act.wait_ge(k_scored, UNITS * b2 + w + 1)
                            if w % 4 == 0 and (w >= 8 or guard_first(r)):
                                act.wait_ge(pv_done, 8 * b2 + w // 4 - 1)
                            act.activation(probs[:, w % 8], ps_k[:, w % 2], ACT.Exp,
                                           scale=SCALE).then_inc(exp_done, 1)
                        if h % 4 == 1 and h >= 5:
                            move_o(r, h // 4 - 1)
                    if pass1 and h == HALF + 1:
                        move_max(r, 0, pass2)
                if pass2:
                    move_o(r, GROUPS - 1)
                if pass1:
                    move_max(r, 1, pass2)

            rounds(act, one)

        @block.gpsimd
        def _(pool):
            def split(r, half):
                idx = 2 * r + half
                pool.wait_ge(m_moved, idx + 1)
                pool.tensor_tensor(m_rest[:], m_row[:], m_part[:, half, 0, :],
                                   ALU.subtract).then_inc(m_less, 1)
                pool.tensor_tensor(m_part[:, half, 1, :], m_row[:], m_part[:, half, 0, :],
                                   ALU.subtract).then_inc(m_second, 1)
                pool.wait_ge(m_less, idx + 1)
                pool.wait_ge(m_second, idx + 1)
                pool.tensor_tensor(m_part[:, half, 2, :], m_rest[:], m_part[:, half, 1, :],
                                   ALU.subtract).then_inc(m_split, 1)

            def divide(count):
                pool.wait_ge(n_loaded, 16 * GROUPS * count)
                pool.wait_ge(d_spread, 16 * count)
                pool.tensor_tensor(k.x_feat[:, bass.ds((count - 1) * SEQ, SEQ)], o_num[:], o_den[:],
                                   ALU.mult).then_inc(o_divided, 1)

            def one(r, par, pass1, pass2):
                if guard_first(r):
                    divide(r - 1)
                if pass1:
                    split(r, 0)
                    split(r, 1)

            rounds(pool, one)
            divide(BATCH)
            pool.wait_ge(o_divided, BATCH)


def output(k, w, bias, dst, name):
    nc = k.nc
    with ExitStack() as ctx:
        ps = ctx.enter_context(nc.psum_tensor(f"{name}_ps", [P, BATCH, SEQ], F32))
        multiplied = k.sem(f"{name}_multiplied")
        added = k.sem(f"{name}_added")
        block = ctx.enter_context(nc.Block())

        @block.tensor
        def _(pe):
            for t in range(TILES):
                out = ps[:, t // TPB, (t % TPB) * P:(t % TPB + 1) * P]
                last = pe.matmul(out, k.x_feat[:, t * P:(t + 1) * P], w, start=True, stop=bias is None)
                if bias is not None:
                    last = pe.matmul(out, k.ones_row[:], bias, start=False, stop=True)
                if t % TPB == TPB - 1:
                    last.then_inc(multiplied, 1)

        @block.vector
        def _(dve):
            for b in range(BATCH):
                d = dst[:, b * TPB:(b + 1) * TPB, :].rearrange("p t d -> p (t d)")
                dve.wait_ge(multiplied, b + 1)
                dve.tensor_tensor(d, d, ps[:, b], ALU.add).then_inc(added, 1)
            dve.wait_ge(added, BATCH)


def gate(k, name):
    nc = k.nc
    E = EXPERTS
    with ExitStack() as ctx:
        def sb(n, shape, dt=F32):
            return ctx.enter_context(nc.sbuf_tensor(f"{name}_{n}", shape, dt))

        def sem(n):
            return k.sem(f"{name}_{n}")

        ps = ctx.enter_context(nc.psum_tensor(f"{name}_ps", [P, TILES, E + 2], F32))
        ps_t = ctx.enter_context(nc.psum_tensor(f"{name}_pst", [P, 2, SEQ], F32))
        ps_b = ctx.enter_context(nc.psum_tensor(f"{name}_psb", [P, 4, SEQ], F32))
        logit = sb("logit", [P, TILES, E + 2])
        prob = sb("prob", [P, TILES, E + 2])
        pick = sb("pick", [P, TILES, E])
        best = sb("best", [P, 2, TILES])
        total = sb("total", [P, 2, TILES])
        w_row = sb("w_row", [E + 1, 2, SEQ])
        logits, exped, weighed, turned, w_moved, biased, added, step = map(sem, (
            "logits", "exped", "weighed", "turned", "w_moved", "biased", "added", "step"))
        block = ctx.enter_context(nc.Block())
        SOFT = [(0, slice(0, E)), (1, slice(E, E + 2))]

        @block.tensor
        def _(pe):
            for t in range(TILES):
                pe.matmul(ps[:, t, :], k.x_feat[:, t * P:(t + 1) * P], k.gate_w[:], start=True, stop=False)
                last = pe.matmul(ps[:, t, :], k.ones_row[:], k.gate_b[:], start=False, stop=True)
            last.then_inc(logits, 1)
            pe.wait_ge(weighed, 1)
            for b in range(BATCH):
                if b >= 2:
                    pe.wait_ge(w_moved, b - 1)
                for t in range(TPB):
                    last = pe.transpose(ps_t[0:E + 1, b % 2, t * P:(t + 1) * P],
                                        k.w_token[:, b * TPB + t, :], k.ident[:])
                last.then_inc(turned, 1)
                pe.wait_ge(w_moved, b + 1)
                if b >= 4:
                    pe.wait_ge(added, b - 3)
                for t in range(TPB):
                    last = pe.matmul(ps_b[:, b % 4, t * P:(t + 1) * P], w_row[:, b % 2, t * P:(t + 1) * P],
                                     k.b_down[:], start=True, stop=True)
                last.then_inc(biased, 1)

        @block.scalar
        def _(act):
            act.wait_ge(step, 5)
            act.activation(prob[:], logit[:], ACT.Exp).then_inc(exped, 1)
            for b in range(BATCH):
                act.wait_ge(turned, b + 1)
                if b >= 2:
                    act.wait_ge(biased, b - 1)
                act.copy(w_row[:, b % 2, :], ps_t[0:E + 1, b % 2, :]).then_inc(w_moved, 1)

        @block.vector
        def _(dve):
            n = 0

            def link(ins):
                nonlocal n
                n += 1
                ins.then_inc(step, 1)
                dve.wait_ge(step, n)

            dve.wait_ge(logits, 1)
            link(dve.tensor_copy(logit[:], ps[:]))
            for i, s in SOFT:
                link(dve.tensor_reduce(best[:, i], logit[:, :, s], AX.X, ALU.max))
                link(dve.tensor_tensor(logit[:, :, s], logit[:, :, s],
                                       bcast_free(best[:, i], s.stop - s.start), ALU.subtract))
            dve.wait_ge(exped, 1)
            for i, s in SOFT:
                link(dve.tensor_reduce(total[:, i], prob[:, :, s], AX.X, ALU.add))
            link(dve.reciprocal(total[:], total[:]))
            link(dve.tensor_tensor(prob[:, :, E:], prob[:, :, E:], bcast_free(total[:, 1], 2), ALU.mult))
            rank = k.rank[:].unsqueeze(1).to_broadcast([P, TILES, E])
            link(dve.tensor_scalar(pick[:], prob[:, :, 0:E], 1.0, None, ALU.is_ge))
            link(dve.tensor_tensor(pick[:], pick[:], rank, ALU.mult))
            link(dve.tensor_reduce(best[:, 0], pick[:], AX.X, ALU.max))
            link(dve.tensor_tensor(pick[:], pick[:], bcast_free(best[:, 0], E), ALU.is_equal))
            link(dve.tensor_tensor(total[:, 0], total[:, 0], prob[:, :, E], ALU.mult))
            link(dve.tensor_tensor(k.w_token[:, :, 0:E], pick[:], bcast_free(total[:, 0], E), ALU.mult))
            link(dve.tensor_copy(k.w_token[:, :, E], prob[:, :, E + 1]))
            dve.sem_inc(weighed, 1)
            for b in range(BATCH):
                d = k.y_tok[:, b * TPB:(b + 1) * TPB, :].rearrange("p t d -> p (t d)")
                dve.wait_ge(biased, b + 1)
                dve.tensor_tensor(d, d, ps_b[:, b % 4], ALU.add).then_inc(added, 1)
            dve.wait_ge(added, BATCH)


def experts(k, name):
    nc = k.nc
    E = EXPERTS + 1
    RING = 3
    with ExitStack() as ctx:
        def sb(n, shape, dt=F32):
            return ctx.enter_context(nc.sbuf_tensor(f"{name}_{n}", shape, dt))

        def sem(n):
            return k.sem(f"{name}_{n}")

        w1 = sb("w1", [P, E, FFN])
        w2 = sb("w2", [P, E, FC, D])
        b1 = sb("b1", [P, E, FC])
        hidden = sb("hidden", [P, RING, FC, SEQ])
        ps_h = ctx.enter_context(nc.psum_tensor(f"{name}_psh", [P, 4, SEQ], F32))
        ps_y = ctx.enter_context(nc.psum_tensor(f"{name}_psy", [P, RING, SEQ], F32))
        w_loaded = [sem(f"w_loaded{e}") for e in range(E)]
        b_loaded, up, gelu, down, summed, halved = map(sem, (
            "b_loaded", "up", "gelu", "down", "summed", "halved"))
        block = ctx.enter_context(nc.Block())

        @block.sync
        def _(sp):
            sp.dma_start(b1[:], k.a["b1"]).then_inc(b_loaded, 16)
            for e in range(E):
                one, two = (k.a["w1"][e], k.a["w2"][e]) if e < E - 1 else (k.a["rw1"], k.a["rw2"])
                sp.dma_start(w1[:, e, :], one).then_inc(w_loaded[e], 16)
                sp.dma_start(w2[:, e], two.rearrange("(c p) d -> p c d", p=P)).then_inc(w_loaded[e], 16)
            for s in w_loaded:
                sp.wait_ge(s, 32)

        @block.tensor
        def _(pe):
            def go_up(b, e, later):
                if e < E:
                    pe.wait_ge(w_loaded[e], 32)
                for c in range(FC):
                    n = e * FC + c
                    if n >= 4 or later:
                        pe.wait_ge(gelu, E * FC * b + n - 3)
                    pe.matmul(ps_h[:, c], w1[:, e, c * P:(c + 1) * P],
                              k.x_feat[:, bass.ds(b * SEQ, SEQ)], start=True, stop=True).then_inc(up, 1)

            def go_down(b, e, later):
                pe.wait_ge(gelu, E * FC * b + FC * (e + 1))
                if e >= RING or later:
                    pe.wait_ge(summed, (E * b + e - RING + 1) * TPB)
                for t in range(TPB):
                    for c in range(FC):
                        last = pe.matmul(ps_y[:, e % RING, t * P:(t + 1) * P],
                                         hidden[:, e % RING, c, t * P:(t + 1) * P],
                                         w2[:, e, c, :], start=(c == 0), stop=(c == FC - 1))
                last.then_inc(down, 1)

            def one(b, later):
                go_up(b, 0, later)
                for e in range(E):
                    if e + 1 < E:
                        go_up(b, e + 1, later)
                    go_down(b, e, later)

            one(0, False)
            with pe.Fori(1, BATCH) as b:
                one(b, True)

        @block.scalar
        def _(act):
            act.wait_ge(b_loaded, 16)

            def one(b, later):
                for e in range(E):
                    if e >= RING or later:
                        act.wait_ge(down, E * b + e - RING + 1)
                    for c in range(FC):
                        act.wait_ge(up, E * FC * b + e * FC + c + 1)
                        act.activation(hidden[:, e % RING, c, :], ps_h[:, c], ACT.Gelu,
                                       bias=b1[:, e, c:c + 1]).then_inc(gelu, 1)

            one(0, False)
            with act.Fori(1, BATCH) as b:
                one(b, True)

        @block.vector
        def _(dve):
            with dve.Fori(0, BATCH) as b:
                for e in range(E):
                    dve.wait_ge(down, E * b + e + 1)
                    if e > 0:
                        dve.wait_ge(summed, (E * b + e) * TPB)
                    for t in range(TPB):
                        y = k.y_tok[:, bass.ds(b * TPB + t, 1), :].rearrange("p t d -> p (t d)")
                        w = k.w_token[:, bass.ds(b * TPB + t, 1), e]
                        dve.scalar_tensor_tensor(out=y, in0=ps_y[:, e % RING, t * P:(t + 1) * P], scalar=w,
                                                 in1=y, op0=ALU.mult, op1=ALU.add).then_inc(summed, 1)
                dve.wait_ge(summed, (E * b + E) * TPB)
                y = k.y_tok[:, bass.ds(b * TPB, TPB), :]
                x = k.x_tok[:, bass.ds(b * TPB, TPB), :]
                dve.scalar_tensor_tensor(out=x, in0=y, scalar=0.5, in1=x, op0=ALU.mult,
                                         op1=ALU.add).then_inc(halved, 1)
            dve.wait_ge(halved, BATCH)


def store(k, out):
    nc = k.nc
    with ExitStack() as ctx:
        stored = k.sem("stored")
        block = ctx.enter_context(nc.Block())

        @block.sync
        def _(sp):
            sp.dma_start(out.rearrange("b (t p) d -> p (b t) d", p=P), k.x_tok[:]).then_inc(stored, 16)
            sp.wait_ge(stored, 16)


def ffn_layer(k, name):
    layernorm(k, k.x_tok, k.y_tok, f"{name}_outer")
    with k.nc.sbuf_tensor(f"{name}_z", [P, TILES, D], F32) as z:
        layernorm(k, k.y_tok, z, f"{name}_ln1")
        to_features(k, z, k.ln[:, 0:1], k.ln[:, 1:2], f"{name}_t1")
    project(k, False, f"{name}_proj")
    attend(k, f"{name}_att")
    output(k, k.w_o[:], k.b_o[:], k.y_tok, f"{name}_out")
    with k.nc.sbuf_tensor(f"{name}_z2", [P, TILES, D], F32) as z:
        layernorm(k, k.y_tok, z, f"{name}_ln2")
        to_features(k, z, k.ln[:, 2:3], k.ln[:, 3:4], f"{name}_t2")
    gate(k, f"{name}_gate")
    experts(k, f"{name}_moe")
    k.end_layer()


def attention_layer(k, name):
    with k.nc.sbuf_tensor(f"{name}_z", [P, TILES, D], F32) as z:
        layernorm(k, k.x_tok, z, f"{name}_ln")
        to_features(k, z, 1.0, 0.0, f"{name}_t")
    project(k, True, f"{name}_proj")
    attend(k, f"{name}_att")
    output(k, k.a_w[:, 5, :], None, k.x_tok, f"{name}_out")
    k.end_layer()


def macaron(nc, args, out):
    with ExitStack() as ctx:
        k = Core(nc, ctx, args)
        setup(k)
        ffn_layer(k, "f0")
        attention_layer(k, "a0")
        ffn_layer(k, "f1")
        store(k, out)


def rope_tables():
    import math

    import numpy as np

    pos = np.arange(SEQ, dtype=np.float32)[:, None]
    freqs = np.exp(np.float32(-math.log(10000.0)) * np.arange(0, DH, 2, dtype=np.float32) / np.float32(DH))
    angles = (pos * freqs.astype(np.float32)).astype(np.float32)
    sin = np.sin(angles).astype(np.float32).T
    cos = np.cos(angles).astype(np.float32).T
    both = np.zeros((2, HEADS, DH // 2, 2, SEQ), np.float32)
    both[0, :, :, 0] = cos
    both[0, :, :, 1] = cos
    both[1, :, :, 0] = -sin
    both[1, :, :, 1] = sin
    return both.reshape(2, P, SEQ)


def kernel(**inputs):
    import numpy as np
    import concourse.bacc as bacc
    from concourse.bass_utils import run_bass_kernel_spmd

    g = {n[len("L0_"):]: np.asarray(a) for n, a in inputs.items()}

    def swapped(w):
        return w.reshape(D // 2, 2, D)[:, ::-1].reshape(D, D)

    wq, wk = g["attn_W_q"], g["attn_W_k"]
    arrays = {
        "x": g["attn_x"],
        "a_w": np.stack([wq.T, swapped(wq).T, wk.T, swapped(wk).T, g["attn_W_v"].T, g["attn_W_o"].T]),
        "rope": rope_tables(),
        "ln": np.stack([g["ffn_ln1_g"], g["ffn_ln1_b"], g["ffn_ln2_g"], g["ffn_ln2_b"]], 1),
        "w_qkv": g["ffn_Wqkv"], "b_qk": g["ffn_bqkv"][:2 * D].reshape(2, D).T,
        "b_v": g["ffn_bqkv"][2 * D:].reshape(1, D),
        "w_o": g["ffn_Wo"], "b_o": g["ffn_bo"].reshape(1, D),
        "gate_w": g["ffn_gate_w"], "coef_w": g["ffn_coef_w"], "coef_b": g["ffn_coef_b"].reshape(1, 2),
        "w1": g["ffn_W1"], "b1": np.stack([*g["ffn_b1"], g["ffn_rb1"]]).reshape(EXPERTS + 1, FC, P).transpose(2, 0, 1), "w2": g["ffn_W2"], "b2": g["ffn_b2"],
        "rw1": g["ffn_rW1"], "rw2": g["ffn_rW2"],
        "rb2": g["ffn_rb2"].reshape(1, D),
    }
    nc = bacc.Bacc("TRN2", target_bir_lowering=False, num_devices=1)
    feeds, args = {}, {}
    for name, a in arrays.items():
        feeds[f"in_{name}"] = np.ascontiguousarray(a)
        args[name] = nc.dram_tensor(f"in_{name}", a.shape, F32, kind="ExternalInput").ap()
    out = nc.dram_tensor("out", (BATCH, SEQ, D), F32, kind="ExternalOutput").ap()
    macaron(nc, args, out)
    r = run_bass_kernel_spmd(nc, [feeds], core_ids=[0])
    return r.results[0]["out"]
```

```python
from contextlib import ExitStack

import concourse.bass as bass
from concourse import mybir

F32 = mybir.dt.float32
BF16 = mybir.dt.bfloat16
I32 = mybir.dt.int32
U32 = mybir.dt.uint32
ALU = mybir.AluOpType
ACT = mybir.ActivationFunctionType
AX = mybir.AxisListType

P = 128
BATCH, SEQ, D = 8, 512, 128
HEADS, DH = 16, 8
TOKENS = BATCH * SEQ
TILES = TOKENS // P
TPB = SEQ // P
EXPERTS, FFN = 8, 512
FC = FFN // P
PARTS = 3
EPS = 1e-5
SCALE = float(DH) ** -0.5

Q_SLOTS = [(0, 3), (0, 2), (0, 1)]
K_SLOTS = [0, 0, 0, 1, 1, 2]
SLOT_ROWS = DH * len(K_SLOTS)
MAX_ROW = 96
VW = DH + 1
HALF = HEADS // 2

ROWS = 256
SLOTS = TOKENS // ROWS + EXPERTS - 1
W2_AT = FFN
B1_AT = W2_AT + FC * D
B2_AT = B1_AT + FC
PACK = B2_AT + D


def guard_first(r):
    return not (isinstance(r, int) and r <= 1)


def bcast_free(ap, n):
    return ap.unsqueeze(2).to_broadcast([ap.shape[0], ap.shape[1], n])


class Core:

    def __init__(self, nc, ctx, args):
        def sb(name, shape, dt=F32):
            return ctx.enter_context(nc.sbuf_tensor(name, shape, dt))

        self.nc, self.a = nc, args
        self.x_tok = sb("x_tok", [P, TILES, D])
        self.y_tok = sb("y_tok", [P, TILES, D])
        self.x_feat = sb("x_feat", [P, TOKENS])
        self.q_stack = [sb(f"q_stack{i}", [P, HEADS, SEQ], BF16) for i in range(2)]
        self.k_stack = [sb(f"k_stack{i}", [P, HEADS, SEQ], BF16) for i in range(2)]
        self.ident = sb("ident", [P, P])
        self.ones_row = sb("ones_row", [1, P])
        self.w_qkv = sb("w_qkv", [P, 3 * D])
        self.b_qk = sb("b_qk", [P, 2])
        self.b_v = sb("b_v", [1, D])
        self.w_o = sb("w_o", [P, D])
        self.b_o = sb("b_o", [1, D])
        self.ln = sb("ln", [P, 4])
        self.a_w = sb("a_w", [P, 6, D])
        self.gate_w = sb("gate_w", [P, EXPERTS + 2])
        self.gate_b = sb("gate_b", [P, EXPERTS + 2])
        self.marks = sb("marks", [P, 2, P])
        self.before_ones = sb("before_ones", [P, P], BF16)
        self.all_ones = sb("all_ones", [P, P], BF16)
        self.rank = sb("rank", [P, EXPERTS])
        self.up_to = sb("up_to", [P, EXPERTS, EXPERTS])
        self.row_marks = sb("row_marks", [P, TOKENS // ROWS])
        self.slot_marks = sb("slot_marks", [1, SLOTS])

        def dram(name, shape, dt):
            return nc.dram_tensor(name, shape, dt).ap()

        self.sems = []

        self.q_dram = dram("q_dram", [BATCH, HEADS, PARTS, DH, SEQ], BF16)
        self.k_dram = dram("k_dram", [BATCH, HEADS, PARTS, DH, SEQ], BF16)
        self.v_dram = dram("v_dram", [BATCH, P, TPB * HEADS * VW], F32)
        self.o_dram = dram("o_dram", [P, TPB * SEQ], F32)
        self.d_dram = dram("d_dram", [HEADS, SEQ], F32)
        self.sorted_dram = dram("sorted_dram", [SLOTS * ROWS, D], F32)
        self.done_dram = dram("done_dram", [SLOTS * ROWS, D], F32)


    def sem(self, name):
        self.sems.append(self.nc.alloc_semaphore(name))
        return self.sems[-1]

    def end_layer(self):
        self.nc.clear_and_free_semaphores(self.sems)
        self.nc.all_engine_barrier()
        self.sems = []


def setup(k):
    nc, a = k.nc, k.a
    with ExitStack() as ctx:
        loaded = k.sem("loaded")
        zeroed = k.sem("zeroed")
        filled = k.sem("filled")
        rows_zeroed = k.sem("rows_zeroed")
        zero = ctx.enter_context(nc.sbuf_tensor("zero", [P, ROWS], F32))
        block = ctx.enter_context(nc.Block())
        loads = [
            (k.x_tok[:], a["x"].rearrange("b (t p) d -> p (b t) d", p=P)),
            (k.w_qkv[:], a["w_qkv"]), (k.b_qk[:], a["b_qk"]),
            (k.b_v[:], a["b_v"]), (k.w_o[:], a["w_o"]), (k.b_o[:], a["b_o"]),
            (k.ln[:], a["ln"]),
            (k.a_w[:], a["a_w"].rearrange("w i o -> i w o")),
            (k.gate_w[:, 0:EXPERTS], a["gate_w"]), (k.gate_w[:, EXPERTS:], a["coef_w"]),
            (k.gate_b[:], a["gate_b"]), (k.marks[:], a["ones"]), (k.rank[:], a["rank"]),
            (k.up_to[:], a["up_to"]), (k.row_marks[:], a["row_marks"]),
            (k.slot_marks[:], a["slot_marks"]),
        ]

        @block.sync
        def _(sp):
            for dst, src in loads:
                sp.dma_start(dst, src).then_inc(loaded, 16)
            sp.wait_ge(zeroed, 2)
            sp.dma_start(k.sorted_dram.rearrange("(a p r) d -> p a (r d)", p=P, r=2),
                         zero[:].unsqueeze(1).to_broadcast([P, SLOTS, ROWS])).then_inc(rows_zeroed, 16)
            sp.wait_ge(loaded, 16 * len(loads))
            sp.wait_ge(rows_zeroed, 16)

        @block.gpsimd
        def _(pool):
            pool.memset(k.ident[:], 0.0).then_inc(filled, 1)
            pool.wait_ge(filled, 1)
            pool.affine_select(out=k.ident[:], in_=k.ident[:], compare_op=ALU.not_equal, fill=1.0,
                               base=0, pattern=[[-1, P]], channel_multiplier=1).then_inc(filled, 1)
            pool.wait_ge(filled, 2)

        @block.vector
        def _(dve):
            dve.memset(k.ones_row[:], 1.0).then_inc(zeroed, 1)
            dve.memset(zero[:], 0.0).then_inc(zeroed, 1)
            for t in (*k.q_stack, *k.k_stack):
                dve.memset(t[:], 0.0).then_inc(zeroed, 1)
            dve.wait_ge(zeroed, 6)
            for t in k.k_stack:
                dve.memset(t[MAX_ROW:MAX_ROW + PARTS, :, :], 1.0).then_inc(zeroed, 1)
            dve.wait_ge(loaded, 16 * len(loads))
            dve.tensor_copy(k.before_ones[:], k.marks[:, 0]).then_inc(zeroed, 1)
            dve.tensor_copy(k.all_ones[:], k.marks[:, 1]).then_inc(zeroed, 1)
            dve.wait_ge(zeroed, 10)


def layernorm(k, src, dst, name):
    nc = k.nc
    C = 4
    TC = TILES // C
    with ExitStack() as ctx:
        def sb(n, shape):
            return ctx.enter_context(nc.sbuf_tensor(f"{name}_{n}", shape, F32))

        total, var, sd, r, t = (sb(n, [P, TILES]) for n in ("total", "var", "sd", "r", "t"))
        square = sb("square", [P, 2, TC, D])
        done, centered, squared, summed, rooted = (
            k.sem(f"{name}_{n}")
            for n in ("done", "centered", "squared", "summed", "rooted"))
        block = ctx.enter_context(nc.Block())

        @block.scalar
        def _(act):
            for c in range(C):
                act.wait_ge(centered, c + 1)
                if c >= 2:
                    act.wait_ge(summed, c - 1)
                act.activation(square[:, c % 2], dst[:, c * TC:(c + 1) * TC, :],
                               ACT.Square).then_inc(squared, 1)
            act.wait_ge(summed, C + 1)
            act.activation(sd[:], var[:], ACT.Sqrt).then_inc(rooted, 1)

        @block.vector
        def _(dve):
            n = 0
            for c in range(C):
                dve.tensor_reduce(total[:, c * TC:(c + 1) * TC], src[:, c * TC:(c + 1) * TC, :],
                                  AX.X, ALU.add).then_inc(done, 1)
            n += C
            dve.wait_ge(done, n)
            dve.tensor_scalar(total[:], total[:], -1.0 / D, None, ALU.mult).then_inc(done, 1)
            n += 1
            dve.wait_ge(done, n)
            for c in range(C):
                s = slice(c * TC, (c + 1) * TC)
                dve.tensor_tensor(dst[:, s, :], src[:, s, :], bcast_free(total[:, s], D),
                                  ALU.add).then_inc(centered, 1)
            for c in range(C):
                dve.wait_ge(squared, c + 1)
                dve.tensor_reduce(var[:, c * TC:(c + 1) * TC], square[:, c % 2], AX.X,
                                  ALU.add).then_inc(summed, 1)
            dve.wait_ge(summed, C)
            dve.tensor_scalar(var[:], var[:], 1.0 / D, EPS, ALU.mult, ALU.add).then_inc(summed, 1)
            dve.wait_ge(summed, C + 1)
            dve.wait_ge(rooted, 1)
            dve.reciprocal(r[:], sd[:]).then_inc(done, 1)
            for out, x0, x1 in ((t, r, r), (t, t, var)):
                n += 1
                dve.wait_ge(done, n)
                dve.tensor_tensor(out[:], x0[:], x1[:], ALU.mult).then_inc(done, 1)
            n += 1
            dve.wait_ge(done, n)
            dve.tensor_scalar(t[:], t[:], -0.5, 1.5, ALU.mult, ALU.add).then_inc(done, 1)
            n += 1
            dve.wait_ge(done, n)
            dve.tensor_tensor(r[:], r[:], t[:], ALU.mult).then_inc(done, 1)
            n += 1
            dve.wait_ge(done, n)
            dve.wait_ge(centered, C)
            for c in range(C):
                s = slice(c * TC, (c + 1) * TC)
                dve.tensor_tensor(dst[:, s, :], dst[:, s, :], bcast_free(r[:, s], D),
                                  ALU.mult).then_inc(done, 1)
            dve.wait_ge(done, n + C)


def to_features(k, src, gain, bias, name):
    nc = k.nc
    with ExitStack() as ctx:
        ps = ctx.enter_context(nc.psum_tensor(f"{name}_ps", [P, BATCH, SEQ], F32))
        turned = k.sem(f"{name}_turned")
        moved = k.sem(f"{name}_moved")
        block = ctx.enter_context(nc.Block())

        @block.tensor
        def _(pe):
            for t in range(TILES):
                last = pe.transpose(ps[:, t // TPB, (t % TPB) * P:(t % TPB + 1) * P], src[:, t, :],
                                    k.ident[:])
                if t % TPB == TPB - 1:
                    last.then_inc(turned, 1)

        @block.scalar
        def _(act):
            for b in range(0, BATCH, 2):
                act.wait_ge(turned, b + 1)
                act.activation(k.x_feat[:, b * SEQ:(b + 1) * SEQ], ps[:, b], ACT.Identity,
                               scale=gain, bias=bias).then_inc(moved, 1)

        @block.vector
        def _(dve):
            for b in range(1, BATCH, 2):
                dve.wait_ge(turned, b + 1)
                dve.tensor_scalar(k.x_feat[:, b * SEQ:(b + 1) * SEQ], ps[:, b], gain, bias,
                                  ALU.mult, ALU.add).then_inc(moved, 1)
            dve.wait_ge(moved, BATCH)


def project(k, rope, name):
    nc = k.nc
    RING = 3
    with ExitStack() as ctx:
        def sb(n, shape, dt=F32):
            return ctx.enter_context(nc.sbuf_tensor(f"{name}_{n}", shape, dt))

        def sem(n):
            return k.sem(f"{name}_{n}")

        ps = ctx.enter_context(nc.psum_tensor(f"{name}_ps", [P, RING, 2, SEQ], F32))
        ps_v = ctx.enter_context(nc.psum_tensor(f"{name}_psv", [P, 2, SEQ], F32))
        full = sb("full", [P, 2, SEQ])
        rest = sb("rest", [P, 2, SEQ])
        part = sb("part", [P, 2, PARTS, SEQ], BF16)
        v_out = sb("v_out", [P, 2, TPB, HEADS, VW])
        projected, taken, whole, first, less1, second, third = map(sem, (
            "projected", "taken", "whole", "first", "less1", "second", "third"))
        v_done, v_moved, v_ones = map(sem, ("v_done", "v_moved", "v_ones"))
        stored, v_stored = ([sem(f"{n}{i}") for i in range(2)] for n in ("stored", "v_stored"))
        if rope:
            table = sb("table", [P, 2, SEQ])
            turn = sb("turn", [P, 2, 2, SEQ])
            t_loaded, rotated = map(sem, ("t_loaded", "rotated"))
        block = ctx.enter_context(nc.Block())
        items = [(b, s) for b in range(BATCH) for s in range(2)]

        @block.sync
        def _(sp):
            if rope:
                sp.dma_start(table[:], k.a["rope"].rearrange("s p t -> p s t")).then_inc(t_loaded, 16)
                sp.wait_ge(t_loaded, 16)
            for n, (b, s) in enumerate(items):
                sp.wait_ge(third, n + 1)
                for i in range(PARTS):
                    sp.dma_start((k.q_dram, k.k_dram)[s][b, :, i],
                                 part[:, n % 2, i, :]).then_inc(stored[n % 2], 16)
                if s == 1:
                    sp.wait_ge(v_moved, b + 1)
                    sp.dma_start(k.v_dram[b], v_out[:, b % 2].rearrange("p t h w -> p (t h w)")
                                 ).then_inc(v_stored[b % 2], 16)
            for i in range(2):
                sp.wait_ge(stored[i], 16 * PARTS * BATCH)
                sp.wait_ge(v_stored[i], 16 * BATCH // 2)

        @block.tensor
        def _(pe):
            for n, (b, s) in enumerate(items):
                x = k.x_feat[:, b * SEQ:(b + 1) * SEQ]
                if n >= RING:
                    pe.wait_ge(taken, n - RING + 1)
                if rope:
                    pe.matmul(ps[:, n % RING, 0], k.a_w[:, 2 * s, :], x, start=True, stop=True)
                    pe.matmul(ps[:, n % RING, 1], k.a_w[:, 2 * s + 1, :], x, start=True,
                              stop=True).then_inc(projected, 1)
                else:
                    pe.matmul(ps[:, n % RING, 0], k.w_qkv[:, s * D:(s + 1) * D], x, start=True,
                              stop=True).then_inc(projected, 1)
                if s == 0:
                    if b >= 2:
                        pe.wait_ge(v_moved, b - 1)
                    for t in range(TPB):
                        out = ps_v[:, b % 2, t * P:(t + 1) * P]
                        xt = x[:, t * P:(t + 1) * P]
                        if rope:
                            last = pe.matmul(out, xt, k.a_w[:, 4, :], start=True, stop=True)
                        else:
                            pe.matmul(out, xt, k.w_qkv[:, 2 * D:], start=True, stop=False)
                            last = pe.matmul(out, k.ones_row[:], k.b_v[:], start=False, stop=True)
                    last.then_inc(v_done, 1)

        @block.scalar
        def _(act):
            def v_move(b):
                act.wait_ge(v_done, b + 1)
                act.wait_ge(v_ones, 1)
                if b >= 2:
                    act.wait_ge(v_stored[b % 2], 16 * (b // 2))
                act.copy(v_out[:, b % 2, :, :, 0:DH],
                         ps_v[:, b % 2].rearrange("p (t h d) -> p t h d", t=TPB, d=DH)
                         ).then_inc(v_moved, 1)

            def make_whole(n):
                act.wait_ge(projected, n + 1)
                if n >= 2:
                    act.wait_ge(less1, n - 1)
                act.activation(full[:, n % 2], ps[:, n % RING, 0], ACT.Identity,
                               bias=k.b_qk[:, n % 2:n % 2 + 1]).then_inc(taken, 1)

            for n, (b, s) in enumerate(items):
                if not rope:
                    make_whole(n)
                    act.wait_ge(taken, n + 1)
                else:
                    act.wait_ge(whole, n + 1)
                if n >= 2:
                    act.wait_ge(stored[n % 2], 16 * PARTS * (n // 2))
                act.copy(part[:, n % 2, 0, :], full[:, n % 2]).then_inc(first, 1)
                if s == 0:
                    v_move(b)
                act.wait_ge(less1, n + 1)
                act.copy(part[:, n % 2, 1, :], rest[:, n % 2]).then_inc(second, 1)

        @block.vector
        def _(dve):
            dve.memset(v_out[:, :, :, :, DH:], 1.0).then_inc(v_ones, 1)
            if rope:
                dve.wait_ge(t_loaded, 16)

            for n in range(len(items)):
                if rope:
                    dve.wait_ge(projected, n + 1)
                    if n >= 2:
                        dve.wait_ge(whole, n - 1)
                    dve.tensor_tensor(turn[:, n % 2, 0], ps[:, n % RING, 0], table[:, 0],
                                      ALU.mult).then_inc(rotated, 1)
                    dve.tensor_tensor(turn[:, n % 2, 1], ps[:, n % RING, 1], table[:, 1],
                                      ALU.mult).then_inc(taken, 1)
                dve.wait_ge(first, n + 1)
                if n >= 2:
                    dve.wait_ge(third, n - 1)
                dve.tensor_tensor(rest[:, n % 2], full[:, n % 2], part[:, n % 2, 0, :],
                                  ALU.subtract).then_inc(less1, 1)

        @block.gpsimd
        def _(pool):
            for n in range(len(items)):
                if rope:
                    pool.wait_ge(rotated, n + 1)
                    pool.wait_ge(taken, n + 1)
                    if n >= 2:
                        pool.wait_ge(less1, n - 1)
                    pool.tensor_tensor(full[:, n % 2], turn[:, n % 2, 0], turn[:, n % 2, 1],
                                       ALU.add).then_inc(whole, 1)
                pool.wait_ge(second, n + 1)
                pool.tensor_tensor(part[:, n % 2, 2, :], rest[:, n % 2], part[:, n % 2, 1, :],
                                   ALU.subtract).then_inc(third, 1)


def attend(k, name):
    nc = k.nc
    UNITS = 2 * HEADS
    GROUPS = HEADS // 4
    MAXES = HEADS * TPB
    HM = MAXES // 2
    RING = 3
    TURN = (HM + TPB, MAXES + 1)
    LOADS = len(Q_SLOTS) + len(K_SLOTS)
    with ExitStack() as ctx:
        def sb(n, shape, dt=F32):
            return ctx.enter_context(nc.sbuf_tensor(f"{name}_{n}", shape, dt))

        def pb(n, shape):
            return ctx.enter_context(nc.psum_tensor(f"{name}_{n}", shape, F32))

        def sem(n):
            return k.sem(f"{name}_{n}")

        ps_q = pb("ps_q", [P, RING, SEQ])
        ps_k = pb("ps_k", [P, 2, 2, SEQ])
        ps_o = pb("ps_o", [P, SEQ])
        probs = sb("probs", [P, 8, 2, SEQ])
        v_sb = [sb(f"v{i}", [P, TPB, HEADS, VW]) for i in range(2)]
        o_sb = sb("o_sb", [P, GROUPS, SEQ])
        o_num = sb("o_num", [P, SEQ])
        o_den = sb("o_den", [P, SEQ])
        den = sb("den", [P, SEQ // DH])
        maxes = sb("maxes", [P, MAXES])
        m_row = sb("m_row", [HM, P])
        m_rest = sb("m_rest", [HM, P])
        m_part = sb("m_part", [HM, 2, PARTS, P], BF16)
        loaded = [sem("loaded0"), sem("loaded1")]
        v_loaded, o_zeroed = map(sem, ("v_loaded", "o_zeroed"))
        q_scored, q_maxed = map(sem, ("q_scored", "q_maxed"))
        m_turned, m_moved, m_first, m_less, m_second, m_split = map(sem, (
            "m_turned", "m_moved", "m_first", "m_less", "m_second", "m_split"))
        m_loaded = [sem("m_loaded0"), sem("m_loaded1")]
        k_scored, exp_done, pv_done, o_moved = map(sem, ("k_scored", "exp_done", "pv_done", "o_moved"))
        o_stored, n_loaded, d_loaded, d_inverted, d_stored, d_spread, o_divided = map(sem, (
            "o_stored", "n_loaded", "d_loaded", "d_inverted", "d_stored", "d_spread", "o_divided"))
        block = ctx.enter_context(nc.Block())

        def rounds(eng, one):
            one(0, 0, True, False)
            one(1, 1, True, True)
            with eng.Fori(1, BATCH // 2 - 1) as i:
                one(2 * i, 0, True, True)
                one(2 * i + 1, 1, True, True)
            one(BATCH - 2, 0, True, True)
            one(BATCH - 1, 1, True, True)
            one(BATCH, 0, False, True)

        def load_stack(sp, b, par, half):
            h = slice(half * HALF, (half + 1) * HALF)
            row = 0
            for p0, np_ in Q_SLOTS:
                sp.dma_start(k.q_stack[par][row:row + np_ * DH, h, :],
                             k.q_dram[b, h, p0:p0 + np_].rearrange("h i d t -> (i d) h t")
                             ).then_inc(loaded[half], 16)
                row += np_ * DH
            for s, p0 in enumerate(K_SLOTS):
                sp.dma_start(k.k_stack[par][s * DH:(s + 1) * DH, h, :],
                             k.k_dram[b, h, p0].rearrange("h d t -> d h t")
                             ).then_inc(loaded[half], 16)

        def load_max(sp, b, par, half):
            sp.wait_ge(m_split, 2 * b + half + 1)
            for i in range(PARTS):
                sp.dma_start(k.q_stack[par][MAX_ROW + i:MAX_ROW + i + 1, half * HALF:(half + 1) * HALF, :],
                             m_part[:, half, i, :]).then_inc(m_loaded[half], 16)

        o_rows = k.o_dram.rearrange("(g c) (j t) -> j g c t", g=4, j=GROUPS)

        def regroup(sp, count):
            sp.wait_ge(o_moved, GROUPS * count)
            sp.dma_start(k.o_dram, o_sb[:].rearrange("p j t -> p (j t)")).then_inc(o_stored, 16)
            sp.wait_ge(o_stored, 16 * count)
            for j in range(GROUPS):
                sp.dma_start(den[32 * j:32 * j + 32, :],
                             o_rows[j, :, DH, :].rearrange("g (c t) -> g c t", c=DH)
                             ).then_inc(d_loaded, 16)
                sp.dma_start(o_num[32 * j:32 * j + 32, :], o_rows[j, :, 0:DH, :]).then_inc(n_loaded, 16)

        def spread(sp, count):
            sp.wait_ge(d_inverted, count)
            sp.dma_start(k.d_dram.rearrange("h (c t) -> (h c) t", c=DH), den[:]).then_inc(d_stored, 16)
            sp.wait_ge(d_stored, 16 * count)
            sp.dma_start(o_den[:], k.d_dram.unsqueeze(1).to_broadcast([HEADS, DH, SEQ])
                         ).then_inc(d_spread, 16)

        @block.sync
        def _(sp):
            load_stack(sp, 0, 0, 0)
            load_stack(sp, 0, 0, 1)

            def one(r, par, pass1, pass2):
                if pass2:
                    load_max(sp, r - 1, 1 - par, 1)
                if pass1:
                    if pass2:
                        sp.wait_ge(v_loaded, 16 * r)
                        sp.wait_ge(pv_done, 8 * r - 8)
                    sp.dma_start(v_sb[par][:].rearrange("p t h w -> p (t h w)"),
                                 k.v_dram[r]).then_inc(v_loaded, 16)
                if guard_first(r):
                    spread(sp, r - 1)
                last = isinstance(r, int) and r >= BATCH - 1
                if not last:
                    if pass2:
                        sp.wait_ge(k_scored, UNITS * r - UNITS + UNITS // 2)
                    else:
                        sp.wait_ge(loaded[0], 16 * LOADS)
                    load_stack(sp, r + 1, 1 - par, 0)
                if pass1:
                    load_max(sp, r, par, 0)
                if not last:
                    if pass2:
                        sp.wait_ge(k_scored, UNITS * r)
                    else:
                        sp.wait_ge(loaded[1], 16 * LOADS)
                    load_stack(sp, r + 1, 1 - par, 1)
                if pass2:
                    regroup(sp, r)

            rounds(sp, one)
            spread(sp, BATCH)

        @block.tensor
        def _(pe):
            def await_slot(r, u, later):
                if u < RING and not later:
                    return
                before = u - RING
                if before % (MAXES + 2) in TURN:
                    pe.wait_ge(m_moved, 2 * r + (1 if before == TURN[0] else 0))
                else:
                    pe.wait_ge(q_maxed, MAXES * r + before + 1 - (before > TURN[0]) + (before < 0))

            def score_queries(r, par, n, later):
                h, t = n // TPB, n % TPB
                u = n + (n >= TURN[0])
                if n == 0:
                    pe.wait_ge(loaded[0], 16 * LOADS * (r + 1))
                if n == HM:
                    pe.wait_ge(loaded[1], 16 * LOADS * (r + 1))
                await_slot(r, u, later)
                pe.matmul(ps_q[:, u % RING], k.q_stack[par][0:MAX_ROW, h, t * P:(t + 1) * P],
                          k.k_stack[par][0:MAX_ROW, h, :], start=True, stop=True).then_inc(q_scored, 1)

            def turn_maxes(r, half, later):
                u = TURN[half]
                await_slot(r, u, later)
                pe.wait_ge(q_maxed, MAXES * r + HM * (half + 1))
                pe.transpose(ps_q[0:HM, u % RING, 0:P], maxes[:, half * HM:(half + 1) * HM],
                             k.ident[:]).then_inc(m_turned, 1)

            def score_keys(r, par, w):
                b2 = r - 1
                j, half, g = w // 8, w % 8 // 4, w % 4
                head = 4 * j + g
                if w == 0:
                    pe.wait_ge(m_loaded[0], 16 * PARTS * r)
                if w == UNITS // 2:
                    pe.wait_ge(m_loaded[1], 16 * PARTS * r)
                if w >= 2 or guard_first(r):
                    pe.wait_ge(exp_done, UNITS * b2 + w - 1)
                for i in range(2):
                    kt = 2 * half + i
                    last = pe.matmul(ps_k[:, w % 2, i], k.k_stack[1 - par][:, head, kt * P:(kt + 1) * P],
                                     k.q_stack[1 - par][:, head, :], start=True, stop=True)
                last.then_inc(k_scored, 1)

            def apply_v(r, par, v, i):
                b2 = r - 1
                j, half = v // 2, v % 2
                if i == 0:
                    pe.wait_ge(exp_done, UNITS * b2 + 4 * v + 4)
                    if v == 0:
                        pe.wait_ge(o_zeroed, 1)
                        pe.wait_ge(v_loaded, 16 * r)
                    if half == 0 and (j > 0 or guard_first(r)):
                        pe.wait_ge(o_moved, GROUPS * b2 + j)
                for g in range(4):
                    last = pe.matmul(
                        ps_o[32 * g:32 * g + VW, :], v_sb[1 - par][:, 2 * half + i, 4 * j + g, :],
                        probs[:, 4 * half + g, i, :], start=(half == 0 and i == 0),
                        stop=(half == 1 and i == 1), tile_position=(0, 32 * g))
                if i == 1:
                    last.then_inc(pv_done, 1)

            def one(r, par, pass1, pass2):
                for h in range(HEADS):
                    for w in (2 * h, 2 * h + 1):
                        if pass2:
                            score_keys(r, par, w)
                        if pass1:
                            score_queries(r, par, 2 * w, pass2)
                            score_queries(r, par, 2 * w + 1, pass2)
                        if pass2 and w >= 4:
                            if w % 2 == 0:
                                apply_v(r, par, w // 4 - 1, w % 4 // 2)
                    if pass1 and h == HALF:
                        turn_maxes(r, 0, pass2)
                if pass2:
                    apply_v(r, par, 7, 0)
                    apply_v(r, par, 7, 1)
                if pass1:
                    turn_maxes(r, 1, pass2)

            rounds(pe, one)

        @block.vector
        def _(dve):
            dve.memset(ps_o[:], 0.0).then_inc(o_zeroed, 1)

            def invert(count):
                dve.wait_ge(d_loaded, 16 * GROUPS * count)
                dve.reciprocal(den[:], den[:]).then_inc(d_inverted, 1)

            def one(r, par, pass1, pass2):
                for n in range(MAXES):
                    if pass1:
                        dve.wait_ge(q_scored, MAXES * r + n + 1)
                        dve.tensor_reduce(maxes[:, n:n + 1], ps_q[:, (n + (n >= TURN[0])) % RING], AX.X,
                                          ALU.max).then_inc(q_maxed, 1)
                    if guard_first(r) and n == 12:
                        invert(r - 1)

            rounds(dve, one)
            invert(BATCH)

        @block.scalar
        def _(act):
            def move_o(r, j):
                b2 = r - 1
                act.wait_ge(pv_done, 8 * b2 + 2 * j + 2)
                if j == 0 and guard_first(r):
                    act.wait_ge(o_divided, b2)
                act.copy(o_sb[:, j, :], ps_o[:]).then_inc(o_moved, 1)

            def move_max(r, half, later):
                act.wait_ge(m_turned, 2 * r + half + 1)
                if half or later:
                    act.wait_ge(m_split, 2 * r + half)
                act.mul(m_row[:], ps_q[0:HM, TURN[half] % RING, 0:P], -1.0).then_inc(m_first, 1)
                if later:
                    act.wait_ge(m_loaded[half], 16 * PARTS * r)
                act.wait_ge(m_first, 2 * r + half + 1)
                act.mul(m_part[:, half, 0, :], ps_q[0:HM, TURN[half] % RING, 0:P],
                        -1.0).then_inc(m_moved, 1)

            def one(r, par, pass1, pass2):
                for h in range(HEADS):
                    if pass2:
                        b2 = r - 1
                        for w in (2 * h, 2 * h + 1):
                            act.wait_ge(k_scored, UNITS * b2 + w + 1)
                            if w % 4 == 0 and (w >= 8 or guard_first(r)):
                                act.wait_ge(pv_done, 8 * b2 + w // 4 - 1)
                            act.activation(probs[:, w % 8], ps_k[:, w % 2], ACT.Exp,
                                           scale=SCALE).then_inc(exp_done, 1)
                        if h % 4 == 1 and h >= 5:
                            move_o(r, h // 4 - 1)
                    if pass1 and h == HALF + 1:
                        move_max(r, 0, pass2)
                if pass2:
                    move_o(r, GROUPS - 1)
                if pass1:
                    move_max(r, 1, pass2)

            rounds(act, one)

        @block.gpsimd
        def _(pool):
            def split(r, half):
                idx = 2 * r + half
                pool.wait_ge(m_moved, idx + 1)
                pool.tensor_tensor(m_rest[:], m_row[:], m_part[:, half, 0, :],
                                   ALU.subtract).then_inc(m_less, 1)
                pool.tensor_tensor(m_part[:, half, 1, :], m_row[:], m_part[:, half, 0, :],
                                   ALU.subtract).then_inc(m_second, 1)
                pool.wait_ge(m_less, idx + 1)
                pool.wait_ge(m_second, idx + 1)
                pool.tensor_tensor(m_part[:, half, 2, :], m_rest[:], m_part[:, half, 1, :],
                                   ALU.subtract).then_inc(m_split, 1)

            def divide(count):
                pool.wait_ge(n_loaded, 16 * GROUPS * count)
                pool.wait_ge(d_spread, 16 * count)
                pool.tensor_tensor(k.x_feat[:, bass.ds((count - 1) * SEQ, SEQ)], o_num[:], o_den[:],
                                   ALU.mult).then_inc(o_divided, 1)

            def one(r, par, pass1, pass2):
                if guard_first(r):
                    divide(r - 1)
                if pass1:
                    split(r, 0)
                    split(r, 1)

            rounds(pool, one)
            divide(BATCH)
            pool.wait_ge(o_divided, BATCH)


def output(k, w, bias, dst, name):
    nc = k.nc
    with ExitStack() as ctx:
        ps = ctx.enter_context(nc.psum_tensor(f"{name}_ps", [P, BATCH, SEQ], F32))
        multiplied = k.sem(f"{name}_multiplied")
        added = k.sem(f"{name}_added")
        block = ctx.enter_context(nc.Block())

        @block.tensor
        def _(pe):
            for t in range(TILES):
                out = ps[:, t // TPB, (t % TPB) * P:(t % TPB + 1) * P]
                last = pe.matmul(out, k.x_feat[:, t * P:(t + 1) * P], w, start=True, stop=bias is None)
                if bias is not None:
                    last = pe.matmul(out, k.ones_row[:], bias, start=False, stop=True)
                if t % TPB == TPB - 1:
                    last.then_inc(multiplied, 1)

        @block.vector
        def _(dve):
            for b in range(BATCH):
                d = dst[:, b * TPB:(b + 1) * TPB, :].rearrange("p t d -> p (t d)")
                dve.wait_ge(multiplied, b + 1)
                dve.tensor_tensor(d, d, ps[:, b], ALU.add).then_inc(added, 1)
            dve.wait_ge(added, BATCH)


def mixture(k, z, name):
    nc = k.nc
    E = EXPERTS
    R = ROWS // P
    W_RING = 4
    STEP = 4
    with ExitStack() as ctx:
        def sb(n, shape, dt=F32):
            return ctx.enter_context(nc.sbuf_tensor(f"{name}_{n}", shape, dt))

        def sem(n):
            return k.sem(f"{name}_{n}")

        ps_l = ctx.enter_context(nc.psum_tensor(f"{name}_psl", [P, 2, SEQ], F32))
        ps_h = ctx.enter_context(nc.psum_tensor(f"{name}_psh", [P, FC, SEQ], F32))
        ps_y = ctx.enter_context(nc.psum_tensor(f"{name}_psy", [P, 2, SEQ], F32))
        logit = sb("logit", [P, TILES, E + 2])
        prob = sb("prob", [P, TILES, E + 2])
        pick = sb("pick", [P, TILES, E])
        pick16 = sb("pick16", [P, TILES, E], BF16)
        best = sb("best", [P, 2, TILES])
        total = sb("total", [P, 2, TILES])
        scan = [sb(f"scan{i}", [P, TILES, E]) for i in range(2)]
        n_tiles = sb("n_tiles", [P, E])
        ends = sb("ends", [P, E])
        over = sb("over", [P, E, TOKENS // ROWS])
        upto = sb("upto", [P, E, E])
        n_past = sb("n_past", [1, SLOTS])
        past = sb("past", [1, SLOTS, E])
        tile_expert = sb("tile_expert", [1, SLOTS], I32)
        position = sb("position", [P, TILES], U32)
        w_best = sb("w_best", [P, TILES])
        w_res = sb("w_res", [P, TILES])
        res_bias = sb("res_bias", [P, TILES // 2, D])
        res = sb("res", [P, PACK])
        weights = sb("weights", [P, W_RING, PACK])
        rows_in = sb("rows_in", [P, W_RING, R, D])
        feat = sb("feat", [P, 2, ROWS])
        hidden = sb("hidden", [P, 2, FC, SEQ])
        rows_out = sb("rows_out", [P, W_RING, R, D])
        gathered = z
        res_loaded, logits, exped, picked, counted, routed, scattered, res_ready, step = map(sem, (
            "res_loaded", "logits", "exped", "picked", "counted", "routed", "scattered", "res_ready",
            "step"))
        r_bias, r_based, r_up, r_gelu, r_down, r_added = map(sem, (
            "r_bias", "r_based", "r_up", "r_gelu", "r_down", "r_added"))
        turned, moved, up, gelu, down, out_moved, summed, halved = map(sem, (
            "turned", "moved", "up", "gelu", "down", "out_moved", "summed", "halved"))
        in_loaded, out_stored = ([sem(f"{n}{i}") for i in range(W_RING)]
                                 for n in ("in_loaded", "out_stored"))
        fetched = [sem(f"fetched{b}") for b in range(BATCH)]
        block = ctx.enter_context(nc.Block())
        SOFT = [(0, slice(0, E)), (1, slice(E, E + 2))]

        def w1_of(pack, c):
            return pack[:, c * P:(c + 1) * P]

        def w2_of(pack, c):
            return pack[:, W2_AT + c * D:W2_AT + (c + 1) * D]

        def b1_of(pack, c):
            return pack[:, B1_AT + c:B1_AT + c + 1]

        def over_slots(eng, one, first):
            turns = SLOTS // STEP
            for n in range(first, STEP):
                one(n, n)
            with eng.Fori(1, turns) as i:
                for j in range(STEP):
                    one(STEP * i + j, j)
            for n in range(turns * STEP, SLOTS):
                one(n, n % STEP)

        def over_batches(eng, one, between=None):
            one(0, 0)
            if between:
                between()
            one(1, 1)
            with eng.Fori(1, BATCH // 2) as i:
                one(2 * i, 0)
                one(2 * i + 1, 1)

        @block.sync
        def _(sp):
            sp.dma_start(res[:], k.a["mlp"][E]).then_inc(res_loaded, 16)

            def fetch_weights(n, s):
                e = sp.value_load(tile_expert[0:1, bass.ds(n, 1)], min_val=0, max_val=E - 1)
                sp.dma_start(weights[:, s, :], k.a["mlp"][bass.ds(e, 1)].rearrange("e p f -> (e p) f")
                             ).then_inc(in_loaded[s], 16)

            def fetch_rows(n, s):
                sp.dma_start(rows_in[:, s], k.sorted_dram[bass.ds(n * ROWS, ROWS), :].rearrange(
                    "(p r) d -> p r d", r=R)).then_inc(in_loaded[s], 16)

            def save_rows(n, s):
                sp.dma_start(k.done_dram[bass.ds(n * ROWS, ROWS), :].rearrange(
                    "(p r) d -> p r d", r=R), rows_out[:, s]).then_inc(out_stored[s], 16)

            sp.wait_ge(routed, 2)
            for n in range(W_RING - 1):
                fetch_weights(n, n)
            sp.wait_ge(scattered, 16 * TILES)
            for n in range(W_RING - 1):
                fetch_rows(n, n)

            def one(n, s):
                before = (s - 1) % W_RING
                if not isinstance(n, int) or n >= 1:
                    sp.wait_ge(out_moved, n)
                if not isinstance(n, int) or n + W_RING - 1 < SLOTS:
                    fetch_weights(n + W_RING - 1, before)
                    fetch_rows(n + W_RING - 1, before)
                if not isinstance(n, int) or n >= 1:
                    save_rows(n - 1, before)

            over_slots(sp, one, 0)
            sp.wait_ge(out_moved, SLOTS)
            save_rows(SLOTS - 1, (SLOTS - 1) % W_RING)

        @block.tensor
        def _(pe):
            for t in range(TILES):
                last = pe.matmul(ps_l[:, 0, t * (E + 2):(t + 1) * (E + 2)], k.x_feat[:, t * P:(t + 1) * P],
                                 k.gate_w[:], start=True, stop=True)
            last.then_inc(logits, 1)

            def res_up(b):
                for c in range(FC):
                    if not isinstance(b, int) or b >= 1:
                        pe.wait_ge(r_gelu, FC * b - FC + c + 1)
                    pe.matmul(ps_h[:, c], w1_of(res, c), k.x_feat[:, bass.ds(b * SEQ, SEQ)],
                              start=True, stop=True).then_inc(r_up, 1)

            def res_down(b, par):
                pe.wait_ge(r_gelu, FC * b + FC)
                if not isinstance(b, int) or b >= 2:
                    pe.wait_ge(r_added, TPB * b - TPB)
                for t in range(TPB):
                    for c in range(FC):
                        last = pe.matmul(ps_y[:, par, t * P:(t + 1) * P], hidden[:, par, c, t * P:(t + 1) * P],
                                         w2_of(res, c), start=(c == 0), stop=(c == FC - 1))
                last.then_inc(r_down, 1)

            def count():
                pe.wait_ge(picked, 1)
                every = pick16[:].rearrange("p t e -> p (t e)")
                pe.matmul(ps_l[:, 1, 0:TILES * E], k.before_ones[:], every, start=True, stop=True)
                pe.matmul(ps_l[:, 1, TILES * E:], k.all_ones[:], every, start=True,
                          stop=True).then_inc(counted, 1)

            pe.wait_ge(res_loaded, 16)
            res_up(0)
            res_up(1)
            res_down(0, 0)
            count()
            res_up(2)
            res_down(1, 1)
            with pe.Fori(1, BATCH // 2 - 1) as i:
                res_up(2 * i + 1)
                res_down(2 * i, 0)
                res_up(2 * i + 2)
                res_down(2 * i + 1, 1)
            res_up(BATCH - 1)
            res_down(BATCH - 2, 0)
            res_down(BATCH - 1, 1)

            def turn(n, s):
                pe.wait_ge(in_loaded[s], 32 * ((n - s) // STEP + 1) if isinstance(n, int)
                           else 32 * n_turn(n, s) + 32)
                if not isinstance(n, int) or n >= 2:
                    pe.wait_ge(moved, n - 1)
                for r in range(R):
                    last = pe.transpose(ps_l[:, s % 2, r * P:(r + 1) * P], rows_in[:, s, r, :], k.ident[:])
                last.then_inc(turned, 1)

            def go_up(n, s):
                pe.wait_ge(moved, n + 1)
                for c in range(FC):
                    if isinstance(n, int) and n < 2:
                        pe.wait_ge(r_gelu, FC * BATCH)
                    elif c % 2 == 0:
                        pe.wait_ge(gelu, FC * n - 2 * FC + c + 2)
                    at = FC * (s % 2) + c
                    last = pe.matmul(ps_h[:, at // 2, at % 2 * ROWS:(at % 2 + 1) * ROWS],
                                     w1_of(weights[:, s], c), feat[:, s % 2, :], start=True, stop=True)
                    if c % 2 == 1:
                        last.then_inc(up, 1)

            def go_down(n, s):
                pe.wait_ge(gelu, FC * n + FC)
                if isinstance(n, int) and n < 2:
                    pe.wait_ge(r_added, TPB * BATCH)
                else:
                    pe.wait_ge(out_moved, n - 1)
                for r in range(R):
                    for c in range(FC):
                        last = pe.matmul(ps_y[:, s % 2, r * P:(r + 1) * P],
                                         hidden[:, s % 2, c, r * P:(r + 1) * P],
                                         w2_of(weights[:, s], c), start=(c == 0), stop=(c == FC - 1))
                last.then_inc(down, 1)

            def n_turn(n, s):
                return (n - s) // STEP

            def one(n, s):
                if not isinstance(n, int) or n + 1 < SLOTS:
                    turn(n + 1, (s + 1) % STEP)
                go_up(n, s)
                if not isinstance(n, int) or n >= 1:
                    go_down(n - 1, (s - 1) % STEP)

            pe.wait_ge(routed, 3)
            turn(0, 0)
            over_slots(pe, one, 0)
            go_down(SLOTS - 1, (SLOTS - 1) % STEP)

        @block.scalar
        def _(act):
            act.wait_ge(step, 5)
            act.activation(prob[:], logit[:], ACT.Exp).then_inc(exped, 1)
            act.wait_ge(res_loaded, 16)

            def res_one(b, par):
                if not isinstance(b, int) or b >= 2:
                    act.wait_ge(r_down, b - 1)
                for c in range(FC):
                    act.wait_ge(r_up, FC * b + c + 1)
                    act.activation(hidden[:, par, c, :], ps_h[:, c], ACT.Gelu,
                                   bias=b1_of(res, c)).then_inc(r_gelu, 1)

            over_batches(act, res_one)
            act.wait_ge(r_down, BATCH)

            def one(n, s):
                if not isinstance(n, int) or n >= 2:
                    act.wait_ge(down, n - 1)
                for c in range(FC):
                    at = FC * (s % 2) + c
                    if c % 2 == 0:
                        act.wait_ge(up, FC // 2 * n + c // 2 + 1)
                    act.activation(hidden[:, s % 2, c, 0:ROWS],
                                   ps_h[:, at // 2, at % 2 * ROWS:(at % 2 + 1) * ROWS], ACT.Gelu,
                                   bias=b1_of(weights[:, s], c)).then_inc(gelu, 1)

            over_slots(act, one, 0)

        @block.vector
        def _(dve):
            n = 0

            def link(ins):
                nonlocal n
                n += 1
                ins.then_inc(step, 1)
                dve.wait_ge(step, n)

            dve.wait_ge(logits, 1)
            for i, s in SOFT:
                bias = k.gate_b[:, s].unsqueeze(1).to_broadcast([P, TILES, s.stop - s.start])
                here = ps_l[:, 0, 0:TILES * (E + 2)].rearrange("p (t e) -> p t e", e=E + 2)[:, :, s]
                if i == 1:
                    link(dve.tensor_tensor(logit[:, :, s], here, bias, ALU.add))
                    here = logit[:, :, s]
                link(dve.tensor_reduce(best[:, i], here, AX.X, ALU.max))
                dve.tensor_tensor(logit[:, :, s], here, bcast_free(best[:, i], s.stop - s.start),
                                  ALU.subtract).then_inc(step, 1)
                n += 1
            dve.wait_ge(exped, 1)
            for i, s in SOFT:
                link(dve.tensor_reduce(total[:, i], prob[:, :, s], AX.X, ALU.add))
            link(dve.reciprocal(total[:], total[:]))
            dve.tensor_tensor(w_res[:], prob[:, :, E + 1], total[:, 1], ALU.mult).then_inc(res_ready, 1)
            link(dve.tensor_tensor(best[:, 1], total[:, 0], total[:, 1], ALU.mult))
            link(dve.tensor_tensor(w_best[:], best[:, 1], prob[:, :, E], ALU.mult))
            rank = k.rank[:].unsqueeze(1).to_broadcast([P, TILES, E])
            link(dve.tensor_scalar(pick[:], prob[:, :, 0:E], 1.0, None, ALU.is_ge))
            link(dve.tensor_tensor(pick[:], pick[:], rank, ALU.mult))
            link(dve.tensor_reduce(best[:, 0], pick[:], AX.X, ALU.max))
            link(dve.tensor_tensor(pick[:], pick[:], bcast_free(best[:, 0], E), ALU.is_equal))
            link(dve.tensor_copy(pick16[:], pick[:]))
            dve.sem_inc(picked, 1)
            dve.wait_ge(counted, 1)
            link(dve.tensor_copy(scan[0][:].rearrange("p t e -> p (t e)"), ps_l[:, 1, TILES * E:]))
            src, dst, shift = scan[0], scan[1], 1
            while shift < TILES:
                dve.tensor_copy(dst[:, 0:shift, :], src[:, 0:shift, :]).then_inc(step, 1)
                n += 1
                link(dve.tensor_tensor(dst[:, shift:, :], src[:, shift:, :], src[:, 0:TILES - shift, :],
                                       ALU.add))
                src, dst, shift = dst, src, 2 * shift
            every = src[:, TILES - 1, :]
            link(dve.tensor_tensor(over[:], bcast_free(every, TOKENS // ROWS),
                                   k.row_marks[:].unsqueeze(1).to_broadcast([P, E, TOKENS // ROWS]),
                                   ALU.is_gt))
            link(dve.tensor_reduce(n_tiles[:], over[:], AX.X, ALU.add))
            link(dve.tensor_tensor(upto[:], n_tiles[:].unsqueeze(1).to_broadcast([P, E, E]), k.up_to[:],
                                   ALU.mult))
            link(dve.tensor_reduce(ends[:], upto[:], AX.X, ALU.add))
            link(dve.tensor_tensor(past[:], ends[0:1, :].unsqueeze(1).to_broadcast([1, SLOTS, E]),
                                   bcast_free(k.slot_marks[:], E), ALU.is_le))
            link(dve.tensor_reduce(n_past[:], past[:], AX.X, ALU.add))
            dve.tensor_scalar(tile_expert[:], n_past[:], float(E - 1), None, ALU.min).then_inc(routed, 1)
            link(dve.tensor_tensor(ends[:], ends[:], n_tiles[:], ALU.subtract))
            link(dve.tensor_scalar(ends[:], ends[:], float(ROWS), None, ALU.mult))
            link(dve.tensor_tensor(dst[:], src[:], ends[:].unsqueeze(1).to_broadcast([P, TILES, E]), ALU.add))
            link(dve.tensor_tensor(dst[:], dst[:], ps_l[:, 1, TILES * E:].rearrange(
                "p (t e) -> p t e", e=E), ALU.subtract))
            link(dve.tensor_tensor(dst[:], dst[:], ps_l[:, 1, 0:TILES * E].rearrange(
                "p (t e) -> p t e", e=E), ALU.add))
            link(dve.tensor_tensor(dst[:], dst[:], pick[:], ALU.mult))
            link(dve.tensor_reduce(best[:, 0], dst[:], AX.X, ALU.add))
            link(dve.tensor_copy(position[:], best[:, 0]))
            dve.sem_inc(routed, 2)
            dve.wait_ge(r_based, 2)

            def add_res(b, par):
                dve.wait_ge(r_down, b + 1)
                for t in range(TPB):
                    y = k.y_tok[:, bass.ds(b * TPB + t, 1), :].rearrange("p t d -> p (t d)")
                    dve.scalar_tensor_tensor(out=y, in0=ps_y[:, par, t * P:(t + 1) * P],
                                             scalar=w_res[:, bass.ds(b * TPB + t, 1)], in1=y,
                                             op0=ALU.mult, op1=ALU.add).then_inc(r_added, 1)

            over_batches(dve, add_res)

            def move_feat(n, s):
                dve.wait_ge(turned, n + 1)
                if not isinstance(n, int) or n >= 2:
                    dve.wait_ge(up, FC // 2 * (n - 1))
                dve.tensor_scalar(feat[:, s % 2, :], ps_l[:, s % 2, 0:ROWS], k.ln[:, 2:3], k.ln[:, 3:4],
                                  ALU.mult, ALU.add).then_inc(moved, 1)

            def move_out(n, s):
                dve.wait_ge(down, n + 1)
                if not isinstance(n, int) or n >= W_RING:
                    dve.wait_ge(out_stored[s], 16 * ((n - s) // STEP))
                b2 = weights[:, s, B2_AT:].unsqueeze(1).to_broadcast([P, R, D])
                dve.tensor_tensor(rows_out[:, s], ps_y[:, s % 2, 0:ROWS].rearrange("p (r d) -> p r d", r=R),
                                  b2, ALU.add).then_inc(out_moved, 1)

            def one(n, s):
                if not isinstance(n, int) or n + 1 < SLOTS:
                    move_feat(n + 1, (s + 1) % STEP)
                if not isinstance(n, int) or n >= 1:
                    move_out(n - 1, (s - 1) % STEP)

            move_feat(0, 0)
            over_slots(dve, one, 0)
            move_out(SLOTS - 1, (SLOTS - 1) % STEP)
            dve.wait_ge(r_added, TPB * BATCH)
            for b in range(BATCH):
                dve.wait_ge(fetched[b], 16 * TPB)
                for t in range(b * TPB, (b + 1) * TPB):
                    dve.scalar_tensor_tensor(out=k.y_tok[:, t, :], in0=gathered[:, t, :],
                                             scalar=w_best[:, t:t + 1], in1=k.y_tok[:, t, :],
                                             op0=ALU.mult, op1=ALU.add).then_inc(summed, 1)
                s = slice(b * TPB, (b + 1) * TPB)
                dve.wait_ge(summed, TPB * (b + 1))
                dve.scalar_tensor_tensor(out=k.x_tok[:, s, :], in0=k.y_tok[:, s, :], scalar=0.5,
                                         in1=k.x_tok[:, s, :], op0=ALU.mult, op1=ALU.add
                                         ).then_inc(halved, 1)
            dve.wait_ge(halved, BATCH)

        @block.gpsimd
        def _(pool):
            pool.wait_ge(res_loaded, 16)
            pool.wait_ge(res_ready, 1)
            for i in range(2):
                s = slice(i * TILES // 2, (i + 1) * TILES // 2)
                if i:
                    pool.wait_ge(r_based, i)
                pool.tensor_tensor(res_bias[:], res[:, B2_AT:].unsqueeze(1).to_broadcast([P, TILES // 2, D]),
                                   bcast_free(w_res[:, s], D), ALU.mult).then_inc(r_bias, 1)
                pool.wait_ge(r_bias, i + 1)
                pool.tensor_tensor(k.y_tok[:, s, :], k.y_tok[:, s, :], res_bias[:],
                                   ALU.add).then_inc(r_based, 1)
            pool.wait_ge(routed, 3)
            for t in range(TILES):
                pool.indirect_dma_start(k.sorted_dram, bass.IndirectOffsetOnAxis(position[:, t:t + 1], 0),
                                        z[:, t, :], None).then_inc(scattered, 16)
            pool.wait_ge(scattered, 16 * TILES)
            for s in range(W_RING):
                pool.wait_ge(out_stored[s], 16 * len(range(s, SLOTS, W_RING)))
            for t in range(TILES):
                pool.indirect_dma_start(gathered[:, t, :], None, k.done_dram,
                                        bass.IndirectOffsetOnAxis(position[:, t:t + 1], 0)
                                        ).then_inc(fetched[t // TPB], 16)


def store(k, out):
    nc = k.nc
    with ExitStack() as ctx:
        stored = k.sem("stored")
        block = ctx.enter_context(nc.Block())

        @block.sync
        def _(sp):
            sp.dma_start(out.rearrange("b (t p) d -> p (b t) d", p=P), k.x_tok[:]).then_inc(stored, 16)
            sp.wait_ge(stored, 16)


def ffn_layer(k, name):
    layernorm(k, k.x_tok, k.y_tok, f"{name}_outer")
    with k.nc.sbuf_tensor(f"{name}_z", [P, TILES, D], F32) as z:
        layernorm(k, k.y_tok, z, f"{name}_ln1")
        to_features(k, z, k.ln[:, 0:1], k.ln[:, 1:2], f"{name}_t1")
    project(k, False, f"{name}_proj")
    attend(k, f"{name}_att")
    output(k, k.w_o[:], k.b_o[:], k.y_tok, f"{name}_out")
    with k.nc.sbuf_tensor(f"{name}_z2", [P, TILES, D], F32) as z:
        layernorm(k, k.y_tok, z, f"{name}_ln2")
        to_features(k, z, k.ln[:, 2:3], k.ln[:, 3:4], f"{name}_t2")
        mixture(k, z, f"{name}_moe")
    k.end_layer()


def attention_layer(k, name):
    with k.nc.sbuf_tensor(f"{name}_z", [P, TILES, D], F32) as z:
        layernorm(k, k.x_tok, z, f"{name}_ln")
        to_features(k, z, 1.0, 0.0, f"{name}_t")
    project(k, True, f"{name}_proj")
    attend(k, f"{name}_att")
    output(k, k.a_w[:, 5, :], None, k.x_tok, f"{name}_out")
    k.end_layer()


def macaron(nc, args, out):
    with ExitStack() as ctx:
        k = Core(nc, ctx, args)
        setup(k)
        ffn_layer(k, "f0")
        attention_layer(k, "a0")
        ffn_layer(k, "f1")
        store(k, out)


def rope_tables():
    import math

    import numpy as np

    pos = np.arange(SEQ, dtype=np.float32)[:, None]
    freqs = np.exp(np.float32(-math.log(10000.0)) * np.arange(0, DH, 2, dtype=np.float32) / np.float32(DH))
    angles = (pos * freqs.astype(np.float32)).astype(np.float32)
    sin = np.sin(angles).astype(np.float32).T
    cos = np.cos(angles).astype(np.float32).T
    both = np.zeros((2, HEADS, DH // 2, 2, SEQ), np.float32)
    both[0, :, :, 0] = cos
    both[0, :, :, 1] = cos
    both[1, :, :, 0] = -sin
    both[1, :, :, 1] = sin
    return both.reshape(2, P, SEQ)


def marks():
    import numpy as np

    f = np.float32
    return {
        "ones": np.stack([np.triu(np.ones((P, P), f), 1), np.ones((P, P), f)], 1),
        "rank": np.tile(np.arange(EXPERTS, 0, -1, dtype=f), (P, 1)),
        "up_to": np.tile(np.tril(np.ones((EXPERTS, EXPERTS), f)), (P, 1, 1)),
        "row_marks": np.tile(np.arange(0, TOKENS, ROWS, dtype=f), (P, 1)),
        "slot_marks": np.arange(SLOTS, dtype=f).reshape(1, SLOTS),
    }


def kernel(**inputs):
    import numpy as np
    import concourse.bacc as bacc
    from concourse.bass_utils import run_bass_kernel_spmd

    g = {n[len("L0_"):]: np.asarray(a) for n, a in inputs.items()}

    def swapped(w):
        return w.reshape(D // 2, 2, D)[:, ::-1].reshape(D, D)

    def packed(w1, b1, w2, b2):
        return np.concatenate([w1, w2.reshape(FC, P, D).transpose(1, 0, 2).reshape(P, FC * D),
                               b1.reshape(FC, P).T, np.tile(b2, (P, 1))], 1)

    wq, wk = g["attn_W_q"], g["attn_W_k"]
    arrays = {
        "x": g["attn_x"],
        "a_w": np.stack([wq.T, swapped(wq).T, wk.T, swapped(wk).T, g["attn_W_v"].T, g["attn_W_o"].T]),
        "rope": rope_tables(),
        "ln": np.stack([g["ffn_ln1_g"], g["ffn_ln1_b"], g["ffn_ln2_g"], g["ffn_ln2_b"]], 1),
        "w_qkv": g["ffn_Wqkv"], "b_qk": g["ffn_bqkv"][:2 * D].reshape(2, D).T,
        "b_v": g["ffn_bqkv"][2 * D:].reshape(1, D),
        "w_o": g["ffn_Wo"], "b_o": g["ffn_bo"].reshape(1, D),
        "gate_w": g["ffn_gate_w"], "coef_w": g["ffn_coef_w"],
        "gate_b": np.tile(np.concatenate([np.zeros(EXPERTS, np.float32), g["ffn_coef_b"]]), (P, 1)),
        "mlp": np.stack([packed(w1, b1, w2, b2) for w1, b1, w2, b2 in zip(
            [*g["ffn_W1"], g["ffn_rW1"]], [*g["ffn_b1"], g["ffn_rb1"]],
            [*g["ffn_W2"], g["ffn_rW2"]], [*g["ffn_b2"], g["ffn_rb2"]])]),
        **marks(),
    }
    nc = bacc.Bacc("TRN2", target_bir_lowering=False, num_devices=1)
    feeds, args = {}, {}
    for name, a in arrays.items():
        feeds[f"in_{name}"] = np.ascontiguousarray(a)
        args[name] = nc.dram_tensor(f"in_{name}", a.shape, F32, kind="ExternalInput").ap()
    out = nc.dram_tensor("out", (BATCH, SEQ, D), F32, kind="ExternalOutput").ap()
    macaron(nc, args, out)
    r = run_bass_kernel_spmd(nc, [feeds], core_ids=[0])
    return r.results[0]["out"]
```

```python
from contextlib import ExitStack

import concourse.bass as bass
from concourse import mybir

F32 = mybir.dt.float32
BF16 = mybir.dt.bfloat16
I32 = mybir.dt.int32
U32 = mybir.dt.uint32
ALU = mybir.AluOpType
ACT = mybir.ActivationFunctionType
AX = mybir.AxisListType

P = 128
BATCH, SEQ, D = 8, 512, 128
HEADS, DH = 16, 8
TOKENS = BATCH * SEQ
TILES = TOKENS // P
TPB = SEQ // P
EXPERTS, FFN = 8, 512
FC = FFN // P
PARTS = 3
CHUNKS = 4
EPS = 1e-5
SCALE = float(DH) ** -0.5

Q_SLOTS = [0, 1, 2, 0, 1, 0]
K_SLOTS = [0, 0, 0, 1, 1, 2]
MAX_ROW = 96
VW = DH + 1
HALF = HEADS // 2

ROWS = 256
SLOTS = TOKENS // ROWS + EXPERTS - 1
NO_TOKEN = 1 << 20
GATE = EXPERTS + 2
W2_AT = FFN
B1_AT = W2_AT + FC * D
B2_AT = B1_AT + FC
PACK = B2_AT + D


def guard_first(r):
    return not (isinstance(r, int) and r <= 1)


def is_first(b):
    return isinstance(b, int) and b == 0


def last_round(r):
    return isinstance(r, int) and r >= BATCH - 1


def bcast_free(ap, n):
    return ap.unsqueeze(2).to_broadcast([ap.shape[0], ap.shape[1], n])


class Core:

    def __init__(self, nc, ctx, args):
        def sb(name, shape, dt=F32):
            return ctx.enter_context(nc.sbuf_tensor(name, shape, dt))

        self.nc, self.a = nc, args
        self.x_tok = sb("x_tok", [P, TILES, D])
        self.y_tok = sb("y_tok", [P, TILES, D])
        self.x_feat = sb("x_feat", [P, TOKENS])
        self.q_stack = [sb(f"q_stack{i}", [P, HEADS, SEQ], BF16) for i in range(2)]
        self.k_stack = [sb(f"k_stack{i}", [P, HEADS, SEQ], BF16) for i in range(2)]
        self.v_sb = [sb(f"v{i}", [P, TPB, HEADS, VW]) for i in range(2)]
        self.maxes = sb("maxes", [P, HEADS * TPB])
        self.ident = sb("ident", [P, P])
        self.w_qkv = sb("w_qkv", [P, 3 * D])
        self.b_qk = sb("b_qk", [P, 2])
        self.b_v = sb("b_v", [P, D])
        self.w_o = sb("w_o", [P, D])
        self.b_o = sb("b_o", [P, D])
        self.ln = sb("ln", [P, 4])
        self.a_w = sb("a_w", [P, 6, D])
        self.res = sb("res", [P, PACK])
        self.gate_w = sb("gate_w", [P, EXPERTS + 2])
        self.gate_b = sb("gate_b", [P, EXPERTS + 2])
        self.marks = sb("marks", [P, 2, P])
        self.before_ones = sb("before_ones", [P, P], BF16)
        self.all_ones = sb("all_ones", [P, P], BF16)
        self.rank = sb("rank", [P, EXPERTS])
        self.up_to = sb("up_to", [P, EXPERTS, EXPERTS])
        self.row_marks = sb("row_marks", [P, TOKENS // ROWS])
        self.slot_marks = sb("slot_marks", [1, SLOTS])

        def dram(name, shape, dt):
            return nc.dram_tensor(name, shape, dt).ap()

        self.sems = []
        self.zero = sb("zero", [P, ROWS // P, D + 1])
        self.ln_loaded = self.sem("ln_loaded")
        self.x_loaded = [self.sem(f"x_loaded{c}") for c in range(CHUNKS)]
        self.rows_zeroed = self.sem("rows_zeroed")

        self.q_dram = dram("q_dram", [BATCH, HEADS, DH, PARTS, SEQ], BF16)
        self.k_dram = dram("k_dram", [BATCH, HEADS, DH, PARTS, SEQ], BF16)
        self.v_dram = dram("v_dram", [BATCH, P, TPB * HEADS * VW], F32)
        self.o_dram = dram("o_dram", [P, TPB * SEQ], F32)
        self.d_dram = dram("d_dram", [HEADS, SEQ], F32)
        self.sorted_dram = [dram(f"sorted_dram{i}", [SLOTS * ROWS, D + 1], F32) for i in range(2)]
        self.done_dram = dram("done_dram", [TOKENS, D], F32)


    def sem(self, name):
        self.sems.append(self.nc.alloc_semaphore(name))
        return self.sems[-1]

    def end_layer(self):
        self.nc.clear_and_free_semaphores(self.sems)
        self.nc.all_engine_barrier()
        self.sems = []


def setup(k):
    nc, a = k.nc, k.a
    with ExitStack() as ctx:
        filled, zeroed = k.sem("filled"), k.sem("zeroed")
        block = ctx.enter_context(nc.Block())

        @block.sync
        def _(sp):
            tokens = a["x"].rearrange("b (t p) d -> p (b t) d", p=P)
            for c, s in enumerate(k.x_loaded):
                chunk = slice(c * TILES // CHUNKS, (c + 1) * TILES // CHUNKS)
                sp.dma_start(k.x_tok[:, chunk, :], tokens[:, chunk, :]).then_inc(s, 16)
                if c == 0:
                    sp.dma_start(k.ln[:], a["ln"]).then_inc(k.ln_loaded, 16)

        @block.gpsimd
        def _(pool):
            pool.memset(k.ident[:], 0.0).then_inc(filled, 1)
            pool.wait_ge(filled, 1)
            pool.affine_select(out=k.ident[:], in_=k.ident[:], compare_op=ALU.not_equal, fill=1.0,
                               base=0, pattern=[[-1, P]], channel_multiplier=1).then_inc(filled, 1)
            pool.wait_ge(filled, 2)

        @block.vector
        def _(dve):
            dve.memset(k.zero[:, :, 0:D], 0.0).then_inc(zeroed, 1)
            dve.memset(k.zero[:, :, D].bitcast(U32), NO_TOKEN).then_inc(zeroed, 1)
            dve.wait_ge(zeroed, 2)


WEIGHT_LOADS = 14


def load_weights(k, loaded, marks_loaded, sp):
    a = k.a
    sp.dma_start(k.marks[:], a["ones"]).then_inc(marks_loaded, 16)
    loads = [
        (k.w_qkv[:], a["w_qkv"]), (k.b_qk[:], a["b_qk"]), (k.b_v[:], a["b_v"]),
        (k.w_o[:], a["w_o"]), (k.b_o[:], a["b_o"]), (k.a_w[:], a["a_w"].rearrange("w i o -> i w o")),
        (k.gate_w[:, 0:EXPERTS], a["gate_w"]), (k.gate_w[:, EXPERTS:], a["coef_w"]),
        (k.res[:], a["mlp"][EXPERTS]), (k.gate_b[:], a["gate_b"]), (k.rank[:], a["rank"]),
        (k.up_to[:], a["up_to"]), (k.row_marks[:], a["row_marks"]), (k.slot_marks[:], a["slot_marks"]),
    ]
    for dst, src in loads:
        sp.dma_start(dst, src).then_inc(loaded, 16)
    for rows in k.sorted_dram:
        sp.dma_start(rows.rearrange("(a p r) d -> p a (r d)", p=P, r=ROWS // P),
                     k.zero[:].rearrange("p r d -> p (r d)").unsqueeze(1).to_broadcast(
                         [P, SLOTS, ROWS // P * (D + 1)])).then_inc(k.rows_zeroed, 16)
    assert len(loads) == WEIGHT_LOADS
    sp.wait_ge(loaded, 16 * WEIGHT_LOADS)


def clear_stacks(k, i, cleared, pool):
    pool.memset(k.q_stack[i][:].bitcast(F32), 0.0).then_inc(cleared, 1)
    pool.memset(k.k_stack[i][:].bitcast(F32), 0.0).then_inc(cleared, 1)
    pool.wait_ge(cleared, 3 * i + 2)
    pool.memset(k.k_stack[i][MAX_ROW:MAX_ROW + PARTS, :, :], 1.0).then_inc(cleared, 1)
    pool.wait_ge(cleared, 3 * i + 3)


def normalize(k, stages, gain, bias, name, first=False, ps_gate=None, shared=None, memory=None):
    nc = k.nc
    C = CHUNKS
    TC = TILES // C
    BC = BATCH // C
    RING = 3 if shared else 6
    ACT_TILES = TC if first else 5
    with ExitStack() as own:
        ctx = memory or own
        def sb(n, shape):
            return ctx.enter_context(nc.sbuf_tensor(f"{name}_{n}", shape, F32))

        ps = ctx.enter_context(nc.psum_tensor(f"{name}_ps", [P, RING, SEQ], F32))
        n_st = len(stages)
        stats = sb("stats", [P, n_st * C, TC, 6])
        total, apart, var, sd, r, t, shift = (
            sb(n, [P, n_st * C, TC]) for n in ("total", "apart", "var", "sd", "r", "t", "shift"))
        extra, step, varied, rooted, ready, applied, applied_too, turned, gated, *moved = (
            k.sem(f"{name}_{n}")
            for n in ("extra", "step", "varied", "rooted", "ready", "applied", "applied_too", "turned",
                      "gated", "moved0", "moved1"))
        if first:
            loaded, marks_loaded, widened = (
                k.sem(f"{name}_{n}") for n in ("loaded", "marks_loaded", "widened"))
        block = shared or ctx.enter_context(nc.Block())
        if n_st == 1:
            jobs = [(0, c) for c in range(C)]
        else:
            jobs = [(0, 0), (0, 1), (0, 2), (1, 0), (0, 3), (1, 1), (1, 2), (1, 3)]
        last_of = {c: j for j, (s, c) in enumerate(jobs) if s == n_st - 1}
        first_of = {c: j for j, (s, c) in enumerate(jobs) if s == 0}

        def when_moved(eng, b):
            eng.wait_ge(moved[b % 2], b // 2 + 1)

        def when_applied(eng, j):
            eng.wait_ge(applied, j + 1)
            if ACT_TILES < TC:
                eng.wait_ge(applied_too, j + 1)

        if first:
            @block.sync
            def _(sp):
                load_weights(k, loaded, marks_loaded, sp)

        @block.gpsimd
        def _(pool):
            if first:
                for i in range(2):
                    clear_stacks(k, i, extra, pool)
                return
            for j, (s, c) in enumerate(jobs):
                src, dst = stages[s]
                pool.wait_ge(ready, j + 1)
                for i in range(ACT_TILES, TC):
                    last = pool.tensor_scalar(dst[:, c * TC + i, 0:D], src[:, c * TC + i, :],
                                              r[:, j, i:i + 1], shift[:, j, i:i + 1], ALU.mult, ALU.add)
                last.then_inc(applied_too, 1)

        def gate_logits(pe, c):
            for b in range(c * BC, (c + 1) * BC):
                when_moved(pe, b)
                for t in range(b * TPB, (b + 1) * TPB):
                    last = pe.matmul(ps_gate[:, t * GATE:(t + 1) * GATE], k.x_feat[:, t * P:(t + 1) * P],
                                     k.gate_w[:], start=True, stop=True)
                last.then_inc(gated, 1)

        @block.tensor
        def _(pe):
            src = stages[-1][1]
            for c in range(C):
                when_applied(pe, last_of[c])
                for b in range(c * BC, (c + 1) * BC):
                    if b >= RING:
                        when_moved(pe, b - RING)
                    for i in range(TPB):
                        last = pe.transpose(ps[:, b % RING, i * P:(i + 1) * P], src[:, b * TPB + i, 0:D],
                                            k.ident[:])
                    last.then_inc(turned, 1)
                if ps_gate is not None and c >= 1:
                    gate_logits(pe, c - 1)
            if ps_gate is not None:
                gate_logits(pe, C - 1)
                pe.wait_ge(gated, BATCH)

        @block.scalar
        def _(act):
            def apply(j):
                s, c = jobs[j]
                src, dst = stages[s]
                act.wait_ge(ready, j + 1)
                for i in range(ACT_TILES):
                    last = act.activation(dst[:, c * TC + i, 0:D], src[:, c * TC + i, :], ACT.Identity,
                                          scale=r[:, j, i:i + 1], bias=shift[:, j, i:i + 1])
                last.then_inc(applied, 1)

            def to_features(b):
                act.wait_ge(turned, b + 1)
                act.activation(k.x_feat[:, b * SEQ:(b + 1) * SEQ], ps[:, b % RING],
                               ACT.Identity, scale=gain, bias=bias).then_inc(moved[0], 1)

            if first:
                act.wait_ge(k.ln_loaded, 16)
            for j in range(len(jobs)):
                act.wait_ge(varied, j + 1)
                act.activation(sd[:, j], var[:, j], ACT.Sqrt).then_inc(rooted, 1)
                if j >= 1:
                    apply(j - 1)
                    if j >= 2 and jobs[j - 2][0] == n_st - 1:
                        to_features(jobs[j - 2][1] * BC)
            apply(len(jobs) - 1)
            to_features((C - 2) * BC)
            to_features((C - 1) * BC)

        @block.vector
        def _(dve):
            n = 0

            def done(ins):
                nonlocal n
                n += 1
                ins.then_inc(step, 1)
                return n

            def after(count):
                dve.wait_ge(step, count)

            def statistics(j):
                s, c = jobs[j]
                src = stages[s][0]
                if s > 0:
                    when_applied(dve, first_of[c])
                elif first:
                    dve.wait_ge(k.x_loaded[c], 16)
                for i in range(TC):
                    last = done(dve.bn_stats(stats[:, j, i, :], src[:, c * TC + i, :]))
                return last

            def roots(j):
                new, old = j < len(jobs), j >= 1
                p = j - 1
                if new:
                    even, odd = stats[:, j, :, 1], stats[:, j, :, 4]
                    after(statistics(j))
                    a1 = done(dve.tensor_tensor(apart[:, j], even, odd, ALU.subtract))
                    a2 = done(dve.tensor_tensor(var[:, j], stats[:, j, :, 2], stats[:, j, :, 5], ALU.add))
                    a3 = done(dve.tensor_tensor(total[:, j], even, odd, ALU.add))
                if old:
                    dve.wait_ge(varied, p + 1)
                    dve.wait_ge(rooted, p + 1)
                    b1 = done(dve.reciprocal(r[:, p], sd[:, p]))
                if new:
                    after(a1)
                    a1 = done(dve.tensor_tensor(apart[:, j], apart[:, j], apart[:, j], ALU.mult))
                if old:
                    after(b1)
                    b1 = done(dve.tensor_tensor(t[:, p], r[:, p], r[:, p], ALU.mult))
                if new:
                    after(max(a1, a2))
                    a1 = done(dve.scalar_tensor_tensor(
                        out=var[:, j], in0=apart[:, j], scalar=float(D // 4), in1=var[:, j],
                        op0=ALU.mult, op1=ALU.add))
                if old:
                    after(b1)
                    b1 = done(dve.tensor_tensor(t[:, p], t[:, p], var[:, p], ALU.mult))
                if new:
                    after(a1)
                    dve.tensor_scalar(var[:, j], var[:, j], 1.0 / D, EPS, ALU.mult, ALU.add
                                      ).then_inc(varied, 1)
                if old:
                    after(b1)
                    b1 = done(dve.tensor_scalar(t[:, p], t[:, p], -0.5, 1.5, ALU.mult, ALU.add))
                    after(b1)
                    b1 = done(dve.tensor_tensor(r[:, p], r[:, p], t[:, p], ALU.mult))
                    after(b1)
                    dve.scalar_tensor_tensor(out=shift[:, p], in0=total[:, p], scalar=-0.5,
                                             in1=r[:, p], op0=ALU.mult, op1=ALU.mult
                                             ).then_inc(ready, 1)

            def to_features(b):
                dve.wait_ge(turned, b + 1)
                dve.tensor_scalar(k.x_feat[:, b * SEQ:(b + 1) * SEQ], ps[:, b % RING],
                                  gain, bias, ALU.mult, ALU.add).then_inc(moved[1], 1)

            if first:
                dve.wait_ge(k.ln_loaded, 16)
            for j in range(len(jobs)):
                roots(j)
                if j >= 3 and jobs[j - 3][0] == n_st - 1:
                    to_features(jobs[j - 3][1] * BC + 1)
            roots(len(jobs))
            late = [c for c in range(C) if last_of[c] > len(jobs) - 4]
            for c in late:
                to_features(c * BC + 1)
            when_moved(dve, BATCH - 2)
            when_moved(dve, BATCH - 1)
            if first:
                dve.wait_ge(marks_loaded, 16)
                dve.tensor_copy(k.before_ones[:], k.marks[:, 0]).then_inc(widened, 1)
                dve.tensor_copy(k.all_ones[:], k.marks[:, 1]).then_inc(widened, 1)
                dve.wait_ge(widened, 2)

    def when_loaded(eng):
        if first:
            eng.wait_ge(loaded, 16 * WEIGHT_LOADS)

    return when_moved, when_loaded


def project(k, rope, loads, name, shared=None, when_moved=None, when_loaded=None):
    nc = k.nc
    RING = 3
    SLOTS = 6
    TURNS = 3
    LAG = 2
    with ExitStack() as ctx:
        def sb(n, shape, dt=F32):
            return ctx.enter_context(nc.sbuf_tensor(f"{name}_{n}", shape, dt))

        def sem(n):
            return k.sem(f"{name}_{n}")

        ps = ctx.enter_context(nc.psum_tensor(f"{name}_ps", [P, RING, 2 if rope else 1, SEQ], F32))
        ps_v = ctx.enter_context(nc.psum_tensor(f"{name}_psv", [P, 2, SEQ], F32))
        full = sb("full", [P, SLOTS, SEQ])
        rest = sb("rest", [P, SLOTS, SEQ])
        part = sb("part", [P, SLOTS, PARTS, SEQ], BF16)
        v_out = sb("v_out", [P, 2, TPB, HEADS, VW])
        projected, taken, whole, first, less1, second, *third = map(sem, (
            "projected", "taken", "whole", "first", "less1", "second", "third0", "third1"))
        v_done, v_moved, v_ones = map(sem, ("v_done", "v_moved", "v_ones"))
        stored = [sem(f"stored{i}") for i in range(SLOTS)]
        v_stored = [sem(f"v_stored{i}") for i in range(2)]
        if rope:
            table = sb("table", [P, 2, SEQ])
            turn = sb("turn", [P, TURNS, 2, SEQ])
            t_loaded = sem("t_loaded")
        block = shared or ctx.enter_context(nc.Block())
        items = [(b, s) for b in range(BATCH) for s in range(2)]
        N = len(items)

        def by_vector(n):
            return rope and n % 2 == 1

        def when_split(eng, n):
            if rope:
                eng.wait_ge(third[n % 2], n // 2 + 1)
            else:
                eng.wait_ge(third[0], n + 1)

        def third_part(eng, n):
            eng.wait_ge(less1, n + 1)
            eng.wait_ge(second, n + 1)
            eng.tensor_tensor(part[:, n % SLOTS, 2, :], rest[:, n % SLOTS], part[:, n % SLOTS, 1, :],
                              ALU.subtract).then_inc(third[by_vector(n)], 1)

        @block.sync
        def _(sp):
            if rope:
                sp.dma_start(table[:], k.a["rope"].rearrange("s p t -> p s t")).then_inc(t_loaded, 16)
            for n, (b, s) in enumerate(items):
                when_split(sp, n)
                sp.dma_start((k.q_dram, k.k_dram)[s][b].rearrange("h d i t -> (h d) i t"),
                             part[:, n % SLOTS]).then_inc(stored[n % SLOTS], 16)
                if s == 1:
                    sp.wait_ge(v_moved, b + 1)
                    sp.dma_start(k.v_dram[b], v_out[:, b % 2].rearrange("p t h w -> p (t h w)")
                                 ).then_inc(v_stored[b % 2], 16)
                if n == SLOTS + 1:
                    sp.wait_ge(stored[0], 16)
                    sp.wait_ge(stored[1], 16)
                    load_parts(k, sp, 0, 0, 0, loads[0])

        @block.tensor
        def _(pe):
            if when_loaded:
                when_loaded(pe)
            for n, (b, s) in enumerate(items):
                x = k.x_feat[:, b * SEQ:(b + 1) * SEQ]
                if when_moved and s == 0:
                    when_moved(pe, b)
                if n >= RING:
                    pe.wait_ge(taken, n - RING + 1)
                if rope:
                    pe.matmul(ps[:, n % RING, 0], k.a_w[:, 2 * s, :], x, start=True, stop=True)
                    pe.matmul(ps[:, n % RING, 1], k.a_w[:, 2 * s + 1, :], x, start=True,
                              stop=True).then_inc(projected, 1)
                else:
                    pe.matmul(ps[:, n % RING, 0], k.w_qkv[:, s * D:(s + 1) * D], x, start=True,
                              stop=True).then_inc(projected, 1)
                if s == 0:
                    if b >= 2:
                        pe.wait_ge(v_moved, b - 1)
                    for t in range(TPB):
                        last = pe.matmul(ps_v[:, b % 2, t * P:(t + 1) * P], x[:, t * P:(t + 1) * P],
                                         k.a_w[:, 4, :] if rope else k.w_qkv[:, 2 * D:],
                                         start=True, stop=True)
                    last.then_inc(v_done, 1)

        def v_slot(eng, b):
            eng.wait_ge(v_done, b + 1)
            eng.wait_ge(v_ones, 1)
            if b >= 2:
                eng.wait_ge(v_stored[b % 2], 16 * (b // 2))

        def v_of(t):
            return t.rearrange("p (t h d) -> p t h d", t=TPB, d=DH)

        def part_slot(eng, n):
            if n >= SLOTS:
                eng.wait_ge(stored[n % SLOTS], 16 * (n // SLOTS))

        @block.scalar
        def _(act):
            if when_loaded:
                when_loaded(act)
            def second_part(n):
                act.wait_ge(less1, n + 1)
                act.copy(part[:, n % SLOTS, 1, :], rest[:, n % SLOTS]).then_inc(second, 1)

            for n, (b, s) in enumerate(items):
                part_slot(act, n)
                if rope:
                    if n >= LAG:
                        second_part(n - LAG)
                    act.wait_ge(whole, n + 1)
                    act.copy(part[:, n % SLOTS, 0, :], full[:, n % SLOTS]).then_inc(first, 1)
                    if s == 1:
                        v_slot(act, b)
                        act.copy(v_out[:, b % 2, :, :, 0:DH], v_of(ps_v[:, b % 2])).then_inc(v_moved, 1)
                else:
                    bias = k.b_qk[:, s:s + 1]
                    act.wait_ge(projected, n + 1)
                    act.activation(part[:, n % SLOTS, 0, :], ps[:, n % RING, 0], ACT.Identity,
                                   bias=bias).then_inc(first, 1)
                    if n >= SLOTS:
                        act.wait_ge(second, n - SLOTS + 1)
                    act.activation(full[:, n % SLOTS], ps[:, n % RING, 0], ACT.Identity,
                                   bias=bias).then_inc(taken, 1)
            if rope:
                for n in range(N - LAG, N):
                    second_part(n)

        @block.vector
        def _(dve):
            if when_loaded:
                when_loaded(dve)
            dve.memset(v_out[:, :, :, :, DH:], 1.0).then_inc(v_ones, 1)
            if rope:
                dve.wait_ge(t_loaded, 16)

            def less_first(n, dst):
                return dve.tensor_tensor(dst, full[:, n % SLOTS], part[:, n % SLOTS, 0, :], ALU.subtract)

            def rests(n):
                dve.wait_ge(first, n + 1)
                if n >= SLOTS:
                    when_split(dve, n - SLOTS)
                less_first(n, rest[:, n % SLOTS]).then_inc(less1, 1)

            for n, (b, s) in enumerate(items):
                if rope:
                    dve.wait_ge(projected, n + 1)
                    if n >= TURNS:
                        dve.wait_ge(whole, n - TURNS + 1)
                    dve.tensor_tensor(turn[:, n % TURNS, 0], ps[:, n % RING, 0], table[:, 0], ALU.mult)
                    dve.tensor_tensor(turn[:, n % TURNS, 1], ps[:, n % RING, 1], table[:, 1],
                                      ALU.mult).then_inc(taken, 1)
                    if n >= LAG:
                        rests(n - LAG)
                    if n > LAG and by_vector(n - LAG - 1):
                        third_part(dve, n - LAG - 1)
                else:
                    dve.wait_ge(taken, n + 1)
                    rests(n)
                    less_first(n, part[:, n % SLOTS, 1, :]).then_inc(second, 1)
                    if s == 1:
                        v_slot(dve, b)
                        dve.tensor_tensor(v_out[:, b % 2, :, :, 0:DH], v_of(ps_v[:, b % 2]),
                                          k.b_v[:].rearrange("p (h d) -> p h d", d=DH).unsqueeze(1
                                          ).to_broadcast([P, TPB, HEADS, DH]), ALU.add
                                          ).then_inc(v_moved, 1)
            if rope:
                for n in range(N - LAG, N):
                    rests(n)
                for n in range(N - LAG - 1, N):
                    if by_vector(n):
                        third_part(dve, n)

        @block.gpsimd
        def _(pool):
            for n in range(N):
                if rope:
                    pool.wait_ge(taken, n + 1)
                    if n >= SLOTS:
                        pool.wait_ge(less1, n - SLOTS + 1)
                    pool.tensor_tensor(full[:, n % SLOTS], turn[:, n % TURNS, 0],
                                       turn[:, n % TURNS, 1], ALU.add).then_inc(whole, 1)
                    if n > LAG and not by_vector(n - LAG - 1):
                        third_part(pool, n - LAG - 1)
                else:
                    third_part(pool, n)
            if rope:
                for n in range(N - LAG - 1, N):
                    if not by_vector(n):
                        third_part(pool, n)

    return [*((st, 16 * len(range(i, N, SLOTS))) for i, st in enumerate(stored)),
            *((st, 16 * BATCH // 2) for st in v_stored)]


def load_parts(k, sp, b, par, half, sem):
    h = slice(half * HALF, (half + 1) * HALF)
    for stack, parts, slots in ((k.q_stack, k.q_dram, Q_SLOTS), (k.k_stack, k.k_dram, K_SLOTS)):
        for s, i in enumerate(slots):
            sp.dma_start(stack[par][s * DH:(s + 1) * DH, h, :],
                         parts[b, h, :, i].rearrange("h d t -> d h t")).then_inc(sem, 16)


def load_v(k, sp, b, par, sem):
    sp.dma_start(k.v_sb[par][:].rearrange("p t h w -> p (t h w)"), k.v_dram[b]).then_inc(sem, 16)


def attend(k, loads, stores, w_out, bias, dst, name):
    nc = k.nc
    UNITS = 2 * HEADS
    GROUPS = HEADS // 4
    MAXES = HEADS * TPB
    HM = MAXES // 2
    RING = 3
    TURN = (HM + TPB + 1, TPB)
    HQ = SEQ // 2
    LAG = 24
    LOADS = len(Q_SLOTS) + len(K_SLOTS)
    with ExitStack() as ctx:
        def sb(n, shape, dt=F32):
            return ctx.enter_context(nc.sbuf_tensor(f"{name}_{n}", shape, dt))

        def pb(n, shape):
            return ctx.enter_context(nc.psum_tensor(f"{name}_{n}", shape, F32))

        def sem(n):
            return k.sem(f"{name}_{n}")

        ps_q = pb("ps_q", [P, RING, SEQ])
        ps_k = pb("ps_k", [P, 2, 2, SEQ])
        ps_o = pb("ps_o", [P, SEQ])
        probs = sb("probs", [P, 8, 2, SEQ])
        v_sb = k.v_sb
        o_sb = sb("o_sb", [P, GROUPS, SEQ])
        o_num = sb("o_num", [P, SEQ])
        o_den = sb("o_den", [P, SEQ])
        den = sb("den", [P, SEQ // DH])
        maxes = k.maxes
        m_row = sb("m_row", [HM, P])
        m_rest = sb("m_rest", [HM, P])
        m_part = sb("m_part", [HM, 2, PARTS, P], BF16)
        *loaded, v_loaded = loads
        o_zeroed = sem("o_zeroed")
        q_scored, q_maxed = map(sem, ("q_scored", "q_maxed"))
        m_turned, m_moved, m_first, m_less, m_second, m_split = map(sem, (
            "m_turned", "m_moved", "m_first", "m_less", "m_second", "m_split"))
        m_loaded = [sem("m_loaded0"), sem("m_loaded1")]
        k_scored, exp_done, pv_done, o_moved = map(sem, ("k_scored", "exp_done", "pv_done", "o_moved"))
        o_stored, n_loaded, d_loaded, d_inverted, d_stored, d_spread, o_free = map(sem, (
            "o_stored", "n_loaded", "d_loaded", "d_inverted", "d_stored", "d_spread", "o_free"))
        biased, out_multiplied, out_added, last_divided = map(sem, (
            "biased", "out_multiplied", "out_added", "last_divided"))
        block = ctx.enter_context(nc.Block())

        def rounds(eng, one):
            one(0, 0, True, False)
            one(1, 1, True, True)
            with eng.Fori(1, BATCH // 2 - 1) as i:
                one(2 * i, 0, True, True)
                one(2 * i + 1, 1, True, True)
            one(BATCH - 2, 0, True, True)
            one(BATCH - 1, 1, True, True)
            one(BATCH, 0, False, True)

        def pass_two(r, par, w, pass1, pass2):
            if w < LAG:
                return (r - 1, 1 - par, w + UNITS - LAG) if pass2 else None
            return (r, par, w - LAG) if pass1 else None

        def unit_of(n):
            return n + (n >= TPB) + (n >= HM + TPB)

        def load_stack(sp, b, par, half):
            load_parts(k, sp, b, par, half, loaded[half])

        def load_max(sp, b, par, half):
            sp.wait_ge(m_split, 2 * b + half + 1)
            for i in range(PARTS):
                sp.dma_start(k.q_stack[par][MAX_ROW + i:MAX_ROW + i + 1, half * HALF:(half + 1) * HALF, :],
                             m_part[:, half, i, :]).then_inc(m_loaded[half], 16)

        o_rows = k.o_dram.rearrange("(g c) (j t) -> j g c t", g=4, j=GROUPS)[:, :, 0:VW, :]

        def store_outputs(sp, count):
            sp.wait_ge(o_moved, GROUPS * count)
            for g in range(4):
                rows = slice(32 * g, 32 * g + VW)
                sp.dma_start(k.o_dram[rows, :], o_sb[rows].rearrange("p j t -> p (j t)")
                             ).then_inc(o_stored, 16)
            sp.wait_ge(o_stored, 16 * 4 * count)

        def regroup(sp, count):
            store_outputs(sp, count)
            for j in range(GROUPS):
                sp.dma_start(den[32 * j:32 * j + 32, :],
                             o_rows[j, :, DH, :].rearrange("g (c t) -> g c t", c=DH)
                             ).then_inc(d_loaded, 16)
            sp.wait_ge(o_free, count)
            for j in range(GROUPS):
                sp.dma_start(o_num[32 * j:32 * j + 32, :], o_rows[j, :, 0:DH, :]).then_inc(n_loaded, 16)

        def spread(sp, count):
            sp.wait_ge(d_inverted, count)
            sp.dma_start(k.d_dram.rearrange("h (c t) -> (h c) t", c=DH), den[:]).then_inc(d_stored, 16)
            sp.wait_ge(d_stored, 16 * count)
            sp.dma_start(o_den[:], k.d_dram.unsqueeze(1).to_broadcast([HEADS, DH, SEQ])
                         ).then_inc(d_spread, 16)

        @block.sync
        def _(sp):
            for sem_, value in stores:
                sp.wait_ge(sem_, value)
            load_stack(sp, 0, 0, 1)
            load_v(k, sp, 0, 0, v_loaded)

            def one(r, par, pass1, pass2):
                if pass2:
                    load_max(sp, r - 1, 1 - par, 1)
                if pass1 and pass2:
                    sp.wait_ge(v_loaded, 16 * r)
                    if guard_first(r):
                        sp.wait_ge(pv_done, 8 * r - 8)
                    load_v(k, sp, r, par, v_loaded)
                if guard_first(r):
                    spread(sp, r - 1)
                if not last_round(r):
                    if pass2:
                        sp.wait_ge(k_scored, UNITS * r - UNITS + UNITS // 2)
                    else:
                        sp.wait_ge(loaded[0], 16 * LOADS)
                    load_stack(sp, r + 1, 1 - par, 0)
                if pass1:
                    load_max(sp, r, par, 0)
                if not last_round(r):
                    if pass2:
                        sp.wait_ge(k_scored, UNITS * r)
                    else:
                        sp.wait_ge(loaded[1], 16 * LOADS)
                    load_stack(sp, r + 1, 1 - par, 1)
                if pass1 and pass2:
                    regroup(sp, r)
            rounds(sp, one)
            store_outputs(sp, BATCH)
            sp.wait_ge(o_free, BATCH)
            for j in range(GROUPS):
                heads = slice(32 * j, 32 * j + 32)
                sp.dma_start(o_den[heads, :], o_rows[j, :, DH:, :].to_broadcast([4, DH, SEQ])
                             ).then_inc(d_spread, 16)
                sp.dma_start(o_num[heads, :], o_rows[j, :, 0:DH, :]).then_inc(n_loaded, 16)

        @block.tensor
        def _(pe):
            def await_slot(r, u, later):
                before = u - RING
                if before == TURN[1] and not later:
                    before -= RING
                if before == TURN[0]:
                    pe.wait_ge(m_moved, 2 * r + 1)
                elif before == TURN[1]:
                    pe.wait_ge(m_moved, 2 * r)
                elif before >= 0 or later:
                    n = before - (before > TURN[1]) - (before > TURN[0])
                    pe.wait_ge(q_maxed, MAXES * r + n + 1)

            def score_queries(r, par, n, later):
                h, t = n // TPB, n % TPB
                u = unit_of(n)
                if n == 0:
                    pe.wait_ge(loaded[0], 16 * LOADS * (r + 1))
                if n == HM:
                    pe.wait_ge(loaded[1], 16 * LOADS * (r + 1))
                await_slot(r, u, later)
                pe.matmul(ps_q[:, u % RING], k.q_stack[par][0:MAX_ROW, h, t * P:(t + 1) * P],
                          k.k_stack[par][0:MAX_ROW, h, :], start=True, stop=True).then_inc(q_scored, 1)

            def turn_maxes(count, half, more):
                pe.wait_ge(q_maxed, MAXES * count - (0 if half else HM) + (2 if more else 0))
                pe.transpose(ps_q[0:HM, TURN[half] % RING, 0:P], maxes[:, half * HM:(half + 1) * HM],
                             k.ident[:]).then_inc(m_turned, 1)

            def score_keys(b2, par, v):
                j, half, g = v // 8, v % 8 // 4, v % 4
                head = 4 * j + g
                if v == 0:
                    pe.wait_ge(m_loaded[0], 16 * PARTS * b2 + 16 * PARTS)
                if v == UNITS // 2:
                    pe.wait_ge(m_loaded[1], 16 * PARTS * b2 + 16 * PARTS)
                if v >= 2 or not is_first(b2):
                    pe.wait_ge(exp_done, UNITS * b2 + v - 1)
                for i in range(2):
                    kt = 2 * half + i
                    last = pe.matmul(ps_k[:, v % 2, i], k.k_stack[par][:, head, kt * P:(kt + 1) * P],
                                     k.q_stack[par][:, head, :], start=True, stop=True)
                last.then_inc(k_scored, 1)

            def apply_v(b2, v_par, v, quarter, later):
                j, half = v // 2, v % 2
                i, q = quarter // 2, slice(quarter % 2 * HQ, (quarter % 2 + 1) * HQ)
                if quarter == 0:
                    pe.wait_ge(exp_done, UNITS * b2 + 4 * v + 4)
                    if v == 0:
                        pe.wait_ge(o_zeroed, 1)
                        pe.wait_ge(v_loaded, 16 * b2 + 16)
                    if half == 0 and (j > 0 or later):
                        pe.wait_ge(o_moved, GROUPS * b2 + j)
                for g in range(4):
                    last = pe.matmul(
                        ps_o[32 * g:32 * g + VW, q], v_sb[v_par][:, 2 * half + i, 4 * j + g, :],
                        probs[:, 4 * half + g, i, q],
                        start=(half == 0 and quarter == 0), stop=(half == 1 and quarter == 3),
                        tile_position=(0, 32 * g))
                if quarter == 3:
                    last.then_inc(pv_done, 1)

            def one(r, par, pass1, pass2):
                for w in range(UNITS):
                    two = pass_two(r, par, w, pass1, pass2)
                    if two:
                        score_keys(*two)
                    if pass1:
                        score_queries(r, par, 2 * w, pass2)
                    late = two and two[2] % 8 == 4
                    if pass1 and late:
                        score_queries(r, par, 2 * w + 1, pass2)
                    if two:
                        b2, par2, v = two
                        if v >= 4:
                            apply_v(b2, par2, v // 4 - 1, v % 4, not is_first(b2))
                        elif pass2:
                            apply_v(r - 1, 1 - par, UNITS // 4 - 1, v, True)
                    if pass1 and not late:
                        score_queries(r, par, 2 * w + 1, pass2)
                    if pass2 and w == 1:
                        turn_maxes(r, 1, pass1)
                    if pass1 and w == HALF * 2 + 1:
                        turn_maxes(r + 1, 0, True)

            rounds(pe, one)
            for quarter in range(4):
                apply_v(BATCH - 1, 1, UNITS // 4 - 1, quarter, True)
            pe.wait_ge(q_maxed, MAXES * BATCH)
            pe.wait_ge(m_moved, 2 * BATCH)
            for b in range(BATCH):
                if b < BATCH - 1:
                    pe.wait_ge(o_free, b + 2)
                else:
                    pe.wait_ge(last_divided, 1)
                if b >= RING:
                    pe.wait_ge(out_added, b - RING + 1)
                for t in range(TPB):
                    at = b * SEQ + t * P
                    last = pe.matmul(ps_q[:, b % RING, t * P:(t + 1) * P], k.x_feat[:, at:at + P], w_out,
                                     start=True, stop=True)
                last.then_inc(out_multiplied, 1)

        @block.vector
        def _(dve):
            dve.memset(ps_o[:], 0.0).then_inc(o_zeroed, 1)

            def invert(count):
                dve.wait_ge(d_loaded, 16 * GROUPS * count)
                dve.reciprocal(den[:], den[:]).then_inc(d_inverted, 1)

            def one(r, par, pass1, pass2):
                for n in range(MAXES):
                    if pass1:
                        dve.wait_ge(q_scored, MAXES * r + n + 1)
                        dve.tensor_reduce(maxes[:, n:n + 1], ps_q[:, unit_of(n) % RING], AX.X,
                                          ALU.max).then_inc(q_maxed, 1)
                    if guard_first(r) and n == 8:
                        invert(r - 1)

            rounds(dve, one)
            if bias is not None:
                dve.wait_ge(biased, 1)
            for b in range(BATCH):
                if b == BATCH - 1:
                    dve.wait_ge(d_spread, 16 * (BATCH - 1 + GROUPS))
                    dve.reciprocal(o_den[:], o_den[:]).then_inc(d_inverted, 1)
                    dve.wait_ge(d_inverted, BATCH)
                    dve.wait_ge(n_loaded, 16 * GROUPS * BATCH)
                    dve.tensor_tensor(k.x_feat[:, (BATCH - 1) * SEQ:], o_num[:], o_den[:],
                                      ALU.mult).then_inc(last_divided, 1)
                d = dst[:, b * TPB:(b + 1) * TPB, :].rearrange("p t d -> p (t d)")
                dve.wait_ge(out_multiplied, b + 1)
                dve.tensor_tensor(d, d, ps_q[:, b % RING], ALU.add).then_inc(out_added, 1)
            dve.wait_ge(out_added, BATCH)

        @block.scalar
        def _(act):
            def move_o(b2, j, later):
                act.wait_ge(pv_done, 8 * b2 + 2 * j + 2)
                if j == 0 and later:
                    act.wait_ge(o_stored, 16 * 4 * b2)
                act.copy(o_sb[:, j, :], ps_o[:]).then_inc(o_moved, 1)

            def move_max(idx, half, later):
                act.wait_ge(m_turned, idx + 1)
                if half or later is not None:
                    act.wait_ge(m_split, idx)
                act.mul(m_row[:], ps_q[0:HM, TURN[half] % RING, 0:P], -1.0).then_inc(m_first, 1)
                if later is not None:
                    act.wait_ge(m_loaded[half], 16 * PARTS * later)
                act.wait_ge(m_first, idx + 1)
                act.mul(m_part[:, half, 0, :], ps_q[0:HM, TURN[half] % RING, 0:P],
                        -1.0).then_inc(m_moved, 1)

            def one(r, par, pass1, pass2):
                for w in range(UNITS):
                    two = pass_two(r, par, w, pass1, pass2)
                    if two:
                        b2, _, v = two
                        later = not is_first(b2)
                        act.wait_ge(k_scored, UNITS * b2 + v + 1)
                        if v % 4 == 0 and (v >= 8 or later):
                            act.wait_ge(pv_done, 8 * b2 + v // 4 - 1)
                        act.activation(probs[:, v % 8], ps_k[:, v % 2], ACT.Exp,
                                       scale=SCALE).then_inc(exp_done, 1)
                        if v % 8 == 3 and v > 8:
                            move_o(b2, v // 8 - 1, later)
                        elif v == 3 and later:
                            move_o(r - 1, GROUPS - 1, True)
                    if pass2 and w == 1:
                        move_max(2 * r - 1, 1, r - 1 if guard_first(r) else None)
                    if pass1 and w == HALF * 2 + 1:
                        move_max(2 * r, 0, r if pass2 else None)

            rounds(act, one)
            move_o(BATCH - 1, GROUPS - 1, True)

        @block.gpsimd
        def _(pool):
            def split(idx, half):
                pool.wait_ge(m_moved, idx + 1)
                pool.tensor_tensor(m_rest[:], m_row[:], m_part[:, half, 0, :],
                                   ALU.subtract).then_inc(m_less, 1)
                pool.tensor_tensor(m_part[:, half, 1, :], m_row[:], m_part[:, half, 0, :],
                                   ALU.subtract).then_inc(m_second, 1)
                pool.wait_ge(m_less, idx + 1)
                pool.wait_ge(m_second, idx + 1)
                pool.tensor_tensor(m_part[:, half, 2, :], m_rest[:], m_part[:, half, 1, :],
                                   ALU.subtract).then_inc(m_split, 1)

            def divide(count):
                pool.wait_ge(n_loaded, 16 * GROUPS * count)
                pool.wait_ge(d_spread, 16 * count)
                pool.tensor_tensor(k.x_feat[:, bass.ds((count - 1) * SEQ, SEQ)], o_num[:], o_den[:],
                                   ALU.mult).then_inc(o_free, 1)

            def one(r, par, pass1, pass2):
                if pass2:
                    split(2 * r - 1, 1)
                if guard_first(r):
                    divide(r - 1)
                if pass1:
                    split(2 * r, 0)

            if bias is not None:
                pool.tensor_tensor(dst[:], dst[:], bias[:].unsqueeze(1).to_broadcast([P, TILES, D]),
                                   ALU.add).then_inc(biased, 1)
                pool.wait_ge(biased, 1)
            pool.sem_inc(o_free, 1)
            rounds(pool, one)
            pool.wait_ge(o_free, BATCH)


def mixture(k, z, ps_l, first, out, name):
    nc = k.nc
    E = EXPERTS
    R = ROWS // P
    sorted_dram = k.sorted_dram[0 if first else 1]
    W_RING = 4
    STEP = 4
    POOL_BATCHES = 2
    with ExitStack() as ctx:
        def sb(n, shape, dt=F32):
            return ctx.enter_context(nc.sbuf_tensor(f"{name}_{n}", shape, dt))

        def sem(n):
            return k.sem(f"{name}_{n}")

        ps_h = ctx.enter_context(nc.psum_tensor(f"{name}_psh", [P, FC, SEQ], F32))
        ps_y = ctx.enter_context(nc.psum_tensor(f"{name}_psy", [P, 2, SEQ], F32))
        logit = sb("logit", [P, TILES, E + 2])
        prob = sb("prob", [P, TILES, E + 2])
        pick = sb("pick", [P, TILES, E])
        pick16 = sb("pick16", [P, TILES, E], BF16)
        best = sb("best", [P, 2, TILES])
        total = sb("total", [P, 2, TILES])
        scan = [sb(f"scan{i}", [P, TILES, E]) for i in range(2)]
        n_tiles = sb("n_tiles", [P, E])
        ends = sb("ends", [P, E])
        over = sb("over", [P, E, TOKENS // ROWS])
        upto = sb("upto", [P, E, E])
        n_past = sb("n_past", [1, SLOTS])
        past = sb("past", [1, SLOTS, E])
        tile_expert = sb("tile_expert", [1, SLOTS], I32)
        position = sb("position", [P, TILES], U32)
        w_best = sb("w_best", [P, TILES])
        w_res = sb("w_res", [P, TILES])
        res_bias = sb("res_bias", [P, TILES // 2, D])
        res = k.res
        weights = sb("weights", [P, W_RING, PACK])
        rows_in = sb("rows_in", [P, W_RING, R, D + 1])
        row_token = sb("row_token", [P, W_RING, R], U32)
        feat = sb("feat", [P, 2, ROWS])
        hidden = sb("hidden", [P, 2, FC, SEQ])
        rows_out = sb("rows_out", [P, W_RING, R, D])
        returned = z
        exped, picked, counted, routed, scattered, res_ready, step = map(sem, (
            "exped", "picked", "counted", "routed", "scattered", "res_ready",
            "step"))
        r_bias, r_based, r_up, r_gelu, r_down, r_added = map(sem, (
            "r_bias", "r_based", "r_up", "r_gelu", "r_down", "r_added"))
        turned, moved, up, gelu, down, out_moved, summed, halved = map(sem, (
            "turned", "moved", "up", "gelu", "down", "out_moved", "summed", "halved"))
        w_loaded, rows_loaded, out_stored = ([sem(f"{n}{i}") for i in range(W_RING)]
                                             for n in ("w_loaded", "rows_loaded", "out_stored"))
        result_stored, numbered, noted, sending, weighed, pool_summed = map(sem, (
            "result_stored", "numbered", "noted", "sending", "weighed", "pool_summed"))
        fetched = [sem(f"fetched{b}") for b in range(BATCH)]
        block = ctx.enter_context(nc.Block())
        SOFT = [(0, slice(0, E)), (1, slice(E, E + 2))]

        def w1_of(pack, c):
            return pack[:, c * P:(c + 1) * P]

        def w2_of(pack, c):
            return pack[:, W2_AT + c * D:W2_AT + (c + 1) * D]

        def b1_of(pack, c):
            return pack[:, B1_AT + c:B1_AT + c + 1]

        def over_slots(eng, one, first):
            turns = SLOTS // STEP
            for n in range(first, STEP):
                one(n, n)
            with eng.Fori(1, turns) as i:
                for j in range(STEP):
                    one(STEP * i + j, j)
            for n in range(turns * STEP, SLOTS):
                one(n, n % STEP)

        def over_batches(eng, one, between=None):
            one(0, 0)
            if between:
                between()
            one(1, 1)
            with eng.Fori(1, BATCH // 2) as i:
                one(2 * i, 0)
                one(2 * i + 1, 1)

        @block.sync
        def _(sp):
            def fetch_weights(n, s):
                e = sp.value_load(tile_expert[0:1, bass.ds(n, 1)], min_val=0, max_val=E - 1)
                sp.dma_start(weights[:, s, :], k.a["mlp"][bass.ds(e, 1)].rearrange("e p f -> (e p) f")
                             ).then_inc(w_loaded[s], 16)

            def fetch_rows(n, s):
                sp.dma_start(rows_in[:, s], sorted_dram[bass.ds(n * ROWS, ROWS), :].rearrange(
                    "(p r) d -> p r d", r=R)).then_inc(rows_loaded[s], 16)

            sp.wait_ge(routed, 2)
            for n in range(W_RING - 1):
                fetch_weights(n, n)
            sp.wait_ge(scattered, 16 * TILES)
            for n in range(W_RING - 1):
                fetch_rows(n, n)

            def one(n, s):
                before = (s - 1) % W_RING
                if not isinstance(n, int) or n >= 1:
                    sp.wait_ge(out_moved, n)
                if not isinstance(n, int) or n + W_RING - 1 < SLOTS:
                    fetch_rows(n + W_RING - 1, before)
                    fetch_weights(n + W_RING - 1, before)

            over_slots(sp, one, 0)
            for s in range(W_RING):
                sp.wait_ge(out_stored[s], 16 * R * len(range(s, SLOTS, W_RING)))
            for b in (*range(BATCH - POOL_BATCHES, BATCH), *range(BATCH - POOL_BATCHES)):
                sp.dma_start(returned[:, b * TPB:(b + 1) * TPB, 0:D],
                             k.done_dram[b * SEQ:(b + 1) * SEQ, :].rearrange("(t p) d -> p t d", p=P)
                             ).then_inc(fetched[b], 16)
            if out is not None:
                for b in range(BATCH):
                    if b < BATCH - POOL_BATCHES:
                        sp.wait_ge(summed, TPB * (b + 1))
                    else:
                        sp.wait_ge(pool_summed, b + 1 - BATCH + POOL_BATCHES)
                    sp.dma_start(out[b].rearrange("(t p) d -> p t d", p=P),
                                 k.x_tok[:, b * TPB:(b + 1) * TPB, :]).then_inc(result_stored, 16)
                sp.wait_ge(result_stored, 16 * BATCH)

        @block.tensor
        def _(pe):
            def res_up(b):
                for c in range(FC):
                    if not isinstance(b, int) or b >= 1:
                        pe.wait_ge(r_gelu, FC * b - FC + c + 1)
                    pe.matmul(ps_h[:, c], w1_of(res, c), k.x_feat[:, bass.ds(b * SEQ, SEQ)],
                              start=True, stop=True).then_inc(r_up, 1)

            def res_down(b, par):
                pe.wait_ge(r_gelu, FC * b + FC)
                if not isinstance(b, int) or b >= 2:
                    pe.wait_ge(r_added, TPB * b - TPB)
                for t in range(TPB):
                    for c in range(FC):
                        last = pe.matmul(ps_y[:, par, t * P:(t + 1) * P], hidden[:, par, c, t * P:(t + 1) * P],
                                         w2_of(res, c), start=(c == 0), stop=(c == FC - 1))
                last.then_inc(r_down, 1)

            def count():
                pe.wait_ge(picked, 1)
                every = pick16[:].rearrange("p t e -> p (t e)")
                pe.matmul(ps_l[:, 1, 0:TILES * E], k.before_ones[:], every, start=True, stop=True)
                pe.matmul(ps_l[:, 1, TILES * E:], k.all_ones[:], every, start=True,
                          stop=True).then_inc(counted, 1)

            res_up(0)
            res_up(1)
            res_down(0, 0)
            count()
            res_up(2)
            res_down(1, 1)
            with pe.Fori(1, BATCH // 2 - 1) as i:
                res_up(2 * i + 1)
                res_down(2 * i, 0)
                res_up(2 * i + 2)
                res_down(2 * i + 1, 1)
            res_up(BATCH - 1)
            res_down(BATCH - 2, 0)
            res_down(BATCH - 1, 1)

            def turn(n, s):
                pe.wait_ge(rows_loaded[s], 16 * ((n - s) // STEP) + 16)
                if not isinstance(n, int) or n >= 2:
                    pe.wait_ge(moved, n - 1)
                for r in range(R):
                    last = pe.transpose(ps_l[:, s % 2, r * P:(r + 1) * P], rows_in[:, s, r, 0:D],
                                        k.ident[:])
                last.then_inc(turned, 1)

            def go_up(n, s):
                pe.wait_ge(w_loaded[s], 16 * ((n - s) // STEP) + 16)
                pe.wait_ge(moved, n + 1)
                for c in range(FC):
                    if isinstance(n, int) and n < 2:
                        pe.wait_ge(r_gelu, FC * BATCH)
                    elif c % 2 == 0:
                        pe.wait_ge(gelu, FC * n - 2 * FC + c + 2)
                    at = FC * (s % 2) + c
                    last = pe.matmul(ps_h[:, at // 2, at % 2 * ROWS:(at % 2 + 1) * ROWS],
                                     w1_of(weights[:, s], c), feat[:, s % 2, :], start=True, stop=True)
                    if c % 2 == 1:
                        last.then_inc(up, 1)

            def go_down(n, s):
                pe.wait_ge(gelu, FC * n + FC)
                if isinstance(n, int) and n < 2:
                    pe.wait_ge(r_added, TPB * BATCH)
                else:
                    pe.wait_ge(out_moved, n - 1)
                for r in range(R):
                    for c in range(FC):
                        last = pe.matmul(ps_y[:, s % 2, r * P:(r + 1) * P],
                                         hidden[:, s % 2, c, r * P:(r + 1) * P],
                                         w2_of(weights[:, s], c), start=(c == 0), stop=(c == FC - 1))
                last.then_inc(down, 1)

            def one(n, s):
                if not isinstance(n, int) or n + 1 < SLOTS:
                    turn(n + 1, (s + 1) % STEP)
                go_up(n, s)
                if not isinstance(n, int) or n >= 1:
                    go_down(n - 1, (s - 1) % STEP)

            pe.wait_ge(routed, 3)
            turn(0, 0)
            over_slots(pe, one, 0)
            go_down(SLOTS - 1, (SLOTS - 1) % STEP)

        @block.scalar
        def _(act):
            act.wait_ge(step, 5)
            act.activation(prob[:], logit[:], ACT.Exp).then_inc(exped, 1)

            def res_one(b, par):
                if not isinstance(b, int) or b >= 2:
                    act.wait_ge(r_down, b - 1)
                for c in range(FC):
                    act.wait_ge(r_up, FC * b + c + 1)
                    act.activation(hidden[:, par, c, :], ps_h[:, c], ACT.Gelu,
                                   bias=b1_of(res, c)).then_inc(r_gelu, 1)

            over_batches(act, res_one)
            act.wait_ge(r_down, BATCH)

            def one(n, s):
                if not isinstance(n, int) or n >= 2:
                    act.wait_ge(down, n - 1)
                for c in range(FC):
                    at = FC * (s % 2) + c
                    if c % 2 == 0:
                        act.wait_ge(up, FC // 2 * n + c // 2 + 1)
                    act.activation(hidden[:, s % 2, c, 0:ROWS],
                                   ps_h[:, at // 2, at % 2 * ROWS:(at % 2 + 1) * ROWS], ACT.Gelu,
                                   bias=b1_of(weights[:, s], c)).then_inc(gelu, 1)

            over_slots(act, one, 0)

        @block.vector
        def _(dve):
            n = 0

            def link(ins):
                nonlocal n
                n += 1
                ins.then_inc(step, 1)
                dve.wait_ge(step, n)

            for i, s in SOFT:
                bias = k.gate_b[:, s].unsqueeze(1).to_broadcast([P, TILES, s.stop - s.start])
                here = ps_l[:, 0, 0:TILES * (E + 2)].rearrange("p (t e) -> p t e", e=E + 2)[:, :, s]
                if i == 1:
                    link(dve.tensor_tensor(logit[:, :, s], here, bias, ALU.add))
                    here = logit[:, :, s]
                link(dve.tensor_reduce(best[:, i], here, AX.X, ALU.max))
                dve.tensor_tensor(logit[:, :, s], here, bcast_free(best[:, i], s.stop - s.start),
                                  ALU.subtract).then_inc(step, 1)
                n += 1
            dve.wait_ge(exped, 1)
            for i, s in SOFT:
                link(dve.tensor_reduce(total[:, i], prob[:, :, s], AX.X, ALU.add))
            link(dve.reciprocal(total[:], total[:]))
            dve.tensor_tensor(w_res[:], prob[:, :, E + 1], total[:, 1], ALU.mult).then_inc(res_ready, 1)
            link(dve.tensor_tensor(best[:, 1], total[:, 0], total[:, 1], ALU.mult))
            link(dve.scalar_tensor_tensor(out=w_best[:], in0=best[:, 1], scalar=0.5, in1=prob[:, :, E],
                                          op0=ALU.mult, op1=ALU.mult))
            rank = k.rank[:].unsqueeze(1).to_broadcast([P, TILES, E])
            link(dve.tensor_reduce(best[:, 0], prob[:, :, 0:E], AX.X, ALU.max))
            link(dve.tensor_tensor(pick[:], prob[:, :, 0:E], bcast_free(best[:, 0], E), ALU.is_ge))
            link(dve.tensor_tensor(pick[:], pick[:], rank, ALU.mult))
            link(dve.tensor_reduce(best[:, 0], pick[:], AX.X, ALU.max))
            link(dve.tensor_tensor(pick[:], pick[:], bcast_free(best[:, 0], E), ALU.is_equal))
            link(dve.tensor_copy(pick16[:], pick[:]))
            dve.sem_inc(picked, 1)
            dve.wait_ge(counted, 1)
            link(dve.tensor_copy(scan[0][:].rearrange("p t e -> p (t e)"), ps_l[:, 1, TILES * E:]))
            src, dst, shift = scan[0], scan[1], 1
            while shift < TILES:
                dve.tensor_copy(dst[:, 0:shift, :], src[:, 0:shift, :]).then_inc(step, 1)
                n += 1
                link(dve.tensor_tensor(dst[:, shift:, :], src[:, shift:, :], src[:, 0:TILES - shift, :],
                                       ALU.add))
                src, dst, shift = dst, src, 2 * shift
            every = src[:, TILES - 1, :]
            link(dve.tensor_tensor(over[:], bcast_free(every, TOKENS // ROWS),
                                   k.row_marks[:].unsqueeze(1).to_broadcast([P, E, TOKENS // ROWS]),
                                   ALU.is_gt))
            link(dve.tensor_reduce(n_tiles[:], over[:], AX.X, ALU.add))
            link(dve.tensor_tensor(upto[:], n_tiles[:].unsqueeze(1).to_broadcast([P, E, E]), k.up_to[:],
                                   ALU.mult))
            link(dve.tensor_reduce(ends[:], upto[:], AX.X, ALU.add))
            link(dve.tensor_tensor(past[:], ends[0:1, :].unsqueeze(1).to_broadcast([1, SLOTS, E]),
                                   bcast_free(k.slot_marks[:], E), ALU.is_le))
            link(dve.tensor_reduce(n_past[:], past[:], AX.X, ALU.add))
            dve.tensor_scalar(tile_expert[:], n_past[:], float(E - 1), None, ALU.min).then_inc(routed, 1)
            link(dve.tensor_tensor(ends[:], ends[:], n_tiles[:], ALU.subtract))
            link(dve.tensor_scalar(ends[:], ends[:], float(ROWS), None, ALU.mult))
            link(dve.tensor_tensor(dst[:], src[:], ends[:].unsqueeze(1).to_broadcast([P, TILES, E]), ALU.add))
            link(dve.tensor_tensor(dst[:], dst[:], ps_l[:, 1, TILES * E:].rearrange(
                "p (t e) -> p t e", e=E), ALU.subtract))
            link(dve.tensor_tensor(dst[:], dst[:], ps_l[:, 1, 0:TILES * E].rearrange(
                "p (t e) -> p t e", e=E), ALU.add))
            link(dve.tensor_tensor(dst[:], dst[:], pick[:], ALU.mult))
            link(dve.tensor_reduce(best[:, 0], dst[:], AX.X, ALU.add))
            link(dve.tensor_copy(position[:], best[:, 0]))
            dve.sem_inc(routed, 2)
            dve.wait_ge(r_based, 2)

            def add_res(b, par):
                dve.wait_ge(r_down, b + 1)
                for t in range(TPB):
                    y = k.y_tok[:, bass.ds(b * TPB + t, 1), :].rearrange("p t d -> p (t d)")
                    dve.scalar_tensor_tensor(out=y, in0=ps_y[:, par, t * P:(t + 1) * P],
                                             scalar=w_res[:, bass.ds(b * TPB + t, 1)], in1=y,
                                             op0=ALU.mult, op1=ALU.add).then_inc(r_added, 1)
                dve.wait_ge(r_added, TPB * b + TPB)
                x = k.x_tok[:, bass.ds(b * TPB, TPB), :]
                dve.scalar_tensor_tensor(out=x, in0=k.y_tok[:, bass.ds(b * TPB, TPB), :], scalar=0.5,
                                         in1=x, op0=ALU.mult, op1=ALU.add).then_inc(halved, 1)

            over_batches(dve, add_res)

            def move_feat(n, s):
                dve.wait_ge(turned, n + 1)
                if not isinstance(n, int) or n >= 2:
                    dve.wait_ge(up, FC // 2 * (n - 1))
                if not isinstance(n, int) or n >= W_RING:
                    dve.wait_ge(out_stored[s], 16 * R * ((n - s) // STEP))
                dve.tensor_copy(row_token[:, s, :], rows_in[:, s, :, D].bitcast(U32)).then_inc(noted, 1)
                dve.tensor_scalar(feat[:, s % 2, :], ps_l[:, s % 2, 0:ROWS], k.ln[:, 2:3], k.ln[:, 3:4],
                                  ALU.mult, ALU.add).then_inc(moved, 1)

            def move_out(n, s):
                dve.wait_ge(down, n + 1)
                if not isinstance(n, int) or n >= W_RING:
                    dve.wait_ge(out_stored[s], 16 * R * ((n - s) // STEP))
                b2 = weights[:, s, B2_AT:].unsqueeze(1).to_broadcast([P, R, D])
                dve.tensor_tensor(rows_out[:, s], ps_y[:, s % 2, 0:ROWS].rearrange("p (r d) -> p r d", r=R),
                                  b2, ALU.add).then_inc(out_moved, 1)

            def one(n, s):
                if not isinstance(n, int) or n + 1 < SLOTS:
                    move_feat(n + 1, (s + 1) % STEP)
                if not isinstance(n, int) or n >= 1:
                    move_out(n - 1, (s - 1) % STEP)

            move_feat(0, 0)
            over_slots(dve, one, 0)
            move_out(SLOTS - 1, (SLOTS - 1) % STEP)
            dve.wait_ge(halved, BATCH)
            for b in range(BATCH - POOL_BATCHES):
                dve.wait_ge(fetched[b], 16)
                for t in range(b * TPB, (b + 1) * TPB):
                    dve.scalar_tensor_tensor(out=k.x_tok[:, t, :], in0=returned[:, t, 0:D],
                                             scalar=w_best[:, t:t + 1], in1=k.x_tok[:, t, :],
                                             op0=ALU.mult, op1=ALU.add).then_inc(summed, 1)
            dve.wait_ge(summed, TPB * (BATCH - POOL_BATCHES))

        @block.gpsimd
        def _(pool):
            pool.iota(z[:, :, D].bitcast(U32), [[P, TILES]], base=0, channel_multiplier=1
                      ).then_inc(numbered, 1)
            pool.wait_ge(numbered, 1)
            pool.wait_ge(res_ready, 1)
            for i in range(2):
                s = slice(i * TILES // 2, (i + 1) * TILES // 2)
                if i:
                    pool.wait_ge(r_based, i)
                pool.tensor_tensor(res_bias[:], res[:, B2_AT:].unsqueeze(1).to_broadcast([P, TILES // 2, D]),
                                   bcast_free(w_res[:, s], D), ALU.mult).then_inc(r_bias, 1)
                pool.wait_ge(r_bias, i + 1)
                pool.tensor_tensor(k.y_tok[:, s, :], k.y_tok[:, s, :], res_bias[:],
                                   ALU.add).then_inc(r_based, 1)
            pool.wait_ge(routed, 3)
            if first:
                pool.wait_ge(k.rows_zeroed, 32)
            for t in range(TILES):
                pool.indirect_dma_start(sorted_dram, bass.IndirectOffsetOnAxis(position[:, t:t + 1], 0),
                                        z[:, t, :], None).then_inc(scattered, 16)

            def send_back(n, s):
                pool.wait_ge(out_moved, n + 1)
                pool.sem_inc(sending, 1)
                for r in range(R):
                    pool.indirect_dma_start(
                        k.done_dram, bass.IndirectOffsetOnAxis(row_token[:, s, r:r + 1], 0),
                        rows_out[:, s, r, :], None, bounds_check=TOKENS - 1, oob_is_err=False
                    ).then_inc(out_stored[s], 16)

            over_slots(pool, send_back, 0)
            pool.wait_ge(scattered, 16 * TILES)
            pool.wait_ge(halved, BATCH)
            for i in range(POOL_BATCHES):
                b = BATCH - POOL_BATCHES + i
                s = slice(b * TPB, (b + 1) * TPB)
                pool.wait_ge(fetched[b], 16)
                pool.tensor_tensor(returned[:, s, 0:D], returned[:, s, 0:D], bcast_free(w_best[:, s], D),
                                   ALU.mult).then_inc(weighed, 1)
                pool.wait_ge(weighed, i + 1)
                pool.tensor_tensor(k.x_tok[:, s, :], k.x_tok[:, s, :], returned[:, s, 0:D],
                                   ALU.add).then_inc(pool_summed, 1)
            pool.wait_ge(pool_summed, POOL_BATCHES)


def first_loads(k, name):
    return [k.sem(f"{name}_{n}") for n in ("loaded0", "loaded1", "v_loaded")]


def ffn_layer(k, name, first, out=None):
    loads = first_loads(k, name)
    with ExitStack() as memory:
        z = memory.enter_context(k.nc.sbuf_tensor(f"{name}_z", [P, TILES, D], F32))
        block = memory.enter_context(k.nc.Block())
        waits = normalize(k, [(k.x_tok, k.y_tok), (k.y_tok, z)], k.ln[:, 0:1], k.ln[:, 1:2],
                          f"{name}_ln1", first, shared=block, memory=memory)
        stores = project(k, False, loads, f"{name}_proj", block, *waits)
    attend(k, loads, stores, k.w_o[:], k.b_o, k.y_tok, f"{name}_att")
    with k.nc.sbuf_tensor(f"{name}_z2", [P, TILES, D + 1], F32) as z:
        with k.nc.psum_tensor(f"{name}_psl", [P, 2, SEQ], F32) as ps_l:
            normalize(k, [(k.y_tok, z)], k.ln[:, 2:3], k.ln[:, 3:4], f"{name}_ln2", ps_gate=ps_l[:, 0, :])
            mixture(k, z, ps_l, first, out, f"{name}_moe")
    k.end_layer()


def attention_layer(k, name):
    loads = first_loads(k, name)
    with k.nc.sbuf_tensor(f"{name}_z", [P, TILES, D], F32) as z:
        normalize(k, [(k.x_tok, z)], 1.0, 0.0, f"{name}_ln")
    stores = project(k, True, loads, f"{name}_proj")
    attend(k, loads, stores, k.a_w[:, 5, :], None, k.x_tok, f"{name}_att")
    k.end_layer()


def macaron(nc, args, out):
    with ExitStack() as ctx:
        k = Core(nc, ctx, args)
        setup(k)
        ffn_layer(k, "f0", True)
        attention_layer(k, "a0")
        ffn_layer(k, "f1", False, out)


def rope_tables():
    import math

    import numpy as np

    pos = np.arange(SEQ, dtype=np.float32)[:, None]
    freqs = np.exp(np.float32(-math.log(10000.0)) * np.arange(0, DH, 2, dtype=np.float32) / np.float32(DH))
    angles = (pos * freqs.astype(np.float32)).astype(np.float32)
    sin = np.sin(angles).astype(np.float32).T
    cos = np.cos(angles).astype(np.float32).T
    both = np.zeros((2, HEADS, DH // 2, 2, SEQ), np.float32)
    both[0, :, :, 0] = cos
    both[0, :, :, 1] = cos
    both[1, :, :, 0] = -sin
    both[1, :, :, 1] = sin
    return both.reshape(2, P, SEQ)


def marks():
    import numpy as np

    f = np.float32
    return {
        "ones": np.stack([np.triu(np.ones((P, P), f), 1), np.ones((P, P), f)], 1),
        "rank": np.tile(np.arange(EXPERTS, 0, -1, dtype=f), (P, 1)),
        "up_to": np.tile(np.tril(np.ones((EXPERTS, EXPERTS), f)), (P, 1, 1)),
        "row_marks": np.tile(np.arange(0, TOKENS, ROWS, dtype=f), (P, 1)),
        "slot_marks": np.arange(SLOTS, dtype=f).reshape(1, SLOTS),
    }


def kernel(**inputs):
    import numpy as np
    import concourse.bacc as bacc
    from concourse.bass_utils import run_bass_kernel_spmd

    g = {n[len("L0_"):]: np.asarray(a) for n, a in inputs.items()}

    def swapped(w):
        return w.reshape(D // 2, 2, D)[:, ::-1].reshape(D, D)

    def packed(w1, b1, w2, b2):
        return np.concatenate([w1, w2.reshape(FC, P, D).transpose(1, 0, 2).reshape(P, FC * D),
                               b1.reshape(FC, P).T, np.tile(b2, (P, 1))], 1)

    wq, wk = g["attn_W_q"], g["attn_W_k"]
    arrays = {
        "x": g["attn_x"],
        "a_w": np.stack([wq.T, swapped(wq).T, wk.T, swapped(wk).T, g["attn_W_v"].T, g["attn_W_o"].T]),
        "rope": rope_tables(),
        "ln": np.stack([g["ffn_ln1_g"], g["ffn_ln1_b"], g["ffn_ln2_g"], g["ffn_ln2_b"]], 1),
        "w_qkv": g["ffn_Wqkv"], "b_qk": g["ffn_bqkv"][:2 * D].reshape(2, D).T,
        "b_v": np.tile(g["ffn_bqkv"][2 * D:], (P, 1)),
        "w_o": g["ffn_Wo"], "b_o": np.tile(g["ffn_bo"], (P, 1)),
        "gate_w": g["ffn_gate_w"], "coef_w": g["ffn_coef_w"],
        "gate_b": np.tile(np.concatenate([np.zeros(EXPERTS, np.float32), g["ffn_coef_b"]]), (P, 1)),
        "mlp": np.stack([packed(w1, b1, w2, b2) for w1, b1, w2, b2 in zip(
            [*g["ffn_W1"], g["ffn_rW1"]], [*g["ffn_b1"], g["ffn_rb1"]],
            [*g["ffn_W2"], g["ffn_rW2"]], [*g["ffn_b2"], g["ffn_rb2"]])]),
        **marks(),
    }
    nc = bacc.Bacc("TRN2", target_bir_lowering=False, num_devices=1)
    feeds, args = {}, {}
    for name, a in arrays.items():
        feeds[f"in_{name}"] = np.ascontiguousarray(a)
        args[name] = nc.dram_tensor(f"in_{name}", a.shape, F32, kind="ExternalInput").ap()
    out = nc.dram_tensor("out", (BATCH, SEQ, D), F32, kind="ExternalOutput").ap()
    macaron(nc, args, out)
    r = run_bass_kernel_spmd(nc, [feeds], core_ids=[0])
    return r.results[0]["out"]
```
